# Optimizing a Trainium2 kernel written in Bass

```python
import numpy as np
import jax
import jax.numpy as jnp

def _softmax(x, axis=-1):
    return jax.nn.softmax(x, axis=axis)

def _gelu(x):
    return jax.nn.gelu(x, approximate=True)

def _silu(x):
    return jax.nn.silu(x)

def _sigmoid(x):
    return jax.nn.sigmoid(x)

def _layernorm(x, axis=-1, eps=1e-05):
    m = jnp.mean(x, axis=axis, keepdims=True)
    v = jnp.var(x, axis=axis, keepdims=True)
    return (x - m) / jnp.sqrt(v + eps)

def _scatter_add(tgt, idx, src, axis=0):
    return tgt.at[idx].add(src)

def _segment_sum(src, seg, n):
    return jax.ops.segment_sum(src, seg, n)
kernel_name = 'mk_xattn_ffn_d1_seqx_r2_340537'

def setup_inputs(seed: int=0):
    np.random.seed(seed)
    _w = jnp.asarray

    def _rec_inputs():
        import jax
        import jax.numpy as jnp
        _rk = jax.random.key(seed)
        x = -0.000125 + 0.9999 * jax.random.normal(jax.random.fold_in(_rk, 1), (8, 512, 2048), jnp.float32)
        _lenS = 512 - jax.random.randint(jax.random.fold_in(_rk, 7), (8,), 0, max(1, 512 // 4) + 1, jnp.int32)
        _lenS2 = 512 - jax.random.randint(jax.random.fold_in(_rk, 8), (8,), 0, max(1, 512 // 4) + 1, jnp.int32)
        _ctx_4096P = jax.random.normal(jax.random.fold_in(_rk, 11), (8, 16, 2048), jnp.float32)
        _ctx_4096c = jax.random.dirichlet(jax.random.fold_in(_rk, 511), 0.3 * jnp.ones((16,), jnp.float32), (8, 512))
        _ctx_4096t = jnp.einsum('bsk,bkd->bsd', _ctx_4096c, _ctx_4096P)
        _ctx_4096t = _ctx_4096t * jax.lax.rsqrt(jnp.mean(jnp.square(_ctx_4096t)) + 1e-12) * 0.953939
        ctx_4096 = -1.52775e-05 + 0.999936 * (_ctx_4096t + 0.3 * jax.random.normal(jax.random.fold_in(_rk, 611), (8, 512, 2048), jnp.float32))
        return (x, ctx_4096)
    x, ctx_4096 = _rec_inputs()

    def _L0_xattn_setup():
        import jax, jax.numpy as jnp
        import numpy as np
        H = 8
        C = 2

        def _autocorrelation(Q, K, V):
            B, L, D = Q.shape
            d = D // H
            q = Q.reshape(B, L, H, d).transpose(0, 2, 1, 3)
            k = K.reshape(B, L, H, d).transpose(0, 2, 1, 3)
            v = V.reshape(B, L, H, d).transpose(0, 2, 1, 3)
            qf = jnp.fft.fft(q, axis=2)
            kf = jnp.fft.fft(k, axis=2)
            corr = jnp.fft.ifft(qf * jnp.conj(kf), axis=2).real
            topk = int(C * np.log(L))
            w, idx = jax.lax.top_k(corr.transpose(0, 1, 3, 2), topk)
            w = jax.nn.softmax(w, axis=-1)
            pos = jnp.arange(L)[:, None]
            out = jnp.zeros_like(v)
            for i in range(topk):
                g = jnp.minimum(idx[:, :, None, :, i] + pos, L - 1)
                out = out + w[:, :, None, :, i] * jnp.take_along_axis(v, g, axis=2)
            return out.transpose(0, 2, 1, 3).reshape(B, L, D)
        key = jax.random.key(seed)
        k1, k2, k3 = jax.random.split(key, 3)
        B, L, D = (16, 256, 2048)
        Q = jax.random.normal(k1, (B, L, D), dtype=jnp.float32)
        K = jax.random.normal(k2, (B, L, D), dtype=jnp.float32)
        V = jax.random.normal(k3, (B, L, D), dtype=jnp.float32)
        return {'Q': Q, 'K': K, 'V': V}
    _L0_xattn_all = _L0_xattn_setup()
    _L0_xattn_in = {k: v for k, v in _L0_xattn_all.items() if k in ()}
    del _L0_xattn_all

    def _L0_ffn_setup():
        import jax, jax.numpy as jnp
        import numpy as np
        key = jax.random.key(seed)
        k = jax.random.split(key, 6)
        x = jax.random.normal(k[0], (4, 1024, 2048), jnp.float32)
        W = jax.random.normal(k[1], (2048, 2048), jnp.float32) * 0.02
        bias = jax.random.normal(k[2], (2048,), jnp.float32) * 0.02
        A = jax.random.normal(k[3], (16, 16, 2048), jnp.float32) * 0.02
        Bf = jax.random.normal(k[4], (16, 2048, 16), jnp.float32) * 0.02
        coeffs = jax.random.uniform(k[5], (16,), jnp.float32)
        scales = jnp.full((16,), 0.5, jnp.float32)
        return {'x': x, 'W': W, 'bias': bias, 'A': A, 'Bf': Bf, 'coeffs': coeffs, 'scales': scales}
    _L0_ffn_all = _L0_ffn_setup()
    _L0_ffn_in = {k: v for k, v in _L0_ffn_all.items() if k in ('W', 'bias', 'A', 'Bf', 'coeffs', 'scales')}
    del _L0_ffn_all
    return {'x': x, 'ctx_4096': ctx_4096, 'L0_ffn_W': _L0_ffn_in['W'], 'L0_ffn_bias': _L0_ffn_in['bias'], 'L0_ffn_A': _L0_ffn_in['A'], 'L0_ffn_Bf': _L0_ffn_in['Bf'], 'L0_ffn_coeffs': _L0_ffn_in['coeffs'], 'L0_ffn_scales': _L0_ffn_in['scales']}

def reference(x, ctx_4096, L0_ffn_W, L0_ffn_bias, L0_ffn_A, L0_ffn_Bf, L0_ffn_coeffs, L0_ffn_scales):
    import jax
    import jax.numpy as jnp

    def _L0_xattn_ref(Q, K, V):
        import jax, jax.numpy as jnp
        import numpy as np
        H = 8
        C = 2

        def _autocorrelation(Q, K, V):
            B, L, D = Q.shape
            d = D // H
            q = Q.reshape(B, L, H, d).transpose(0, 2, 1, 3)
            k = K.reshape(B, L, H, d).transpose(0, 2, 1, 3)
            v = V.reshape(B, L, H, d).transpose(0, 2, 1, 3)
            qf = jnp.fft.fft(q, axis=2)
            kf = jnp.fft.fft(k, axis=2)
            corr = jnp.fft.ifft(qf * jnp.conj(kf), axis=2).real
            topk = int(C * np.log(L))
            w, idx = jax.lax.top_k(corr.transpose(0, 1, 3, 2), topk)
            w = jax.nn.softmax(w, axis=-1)
            pos = jnp.arange(L)[:, None]
            out = jnp.zeros_like(v)
            for i in range(topk):
                g = jnp.minimum(idx[:, :, None, :, i] + pos, L - 1)
                out = out + w[:, :, None, :, i] * jnp.take_along_axis(v, g, axis=2)
            return out.transpose(0, 2, 1, 3).reshape(B, L, D)
        return _autocorrelation(Q, K, V)

    def _L0_ffn_ref(x, W, bias, A, Bf, coeffs, scales):
        import jax, jax.numpy as jnp
        import numpy as np
        out = jnp.einsum('bsd,od->bso', x, W) + bias
        xa = jnp.einsum('bsd,erd->ebsr', x, A)
        w = coeffs * scales
        upd = jnp.einsum('ebsr,eor,e->bso', xa, Bf, w)
        return out + upd
    x = x + _L0_xattn_ref(_layernorm(x, axis=-1), ctx_4096, ctx_4096)
    x = x + _L0_ffn_ref(_layernorm(x, axis=-1), L0_ffn_W, L0_ffn_bias, L0_ffn_A, L0_ffn_Bf, L0_ffn_coeffs, L0_ffn_scales)
    return x

_drawn_inputs = setup_inputs


def setup_inputs(seed=0):
    import zlib

    import numpy as np

    out = dict(_drawn_inputs(seed))
    spreads = {'L0_ffn_scales': (0.5, 0.6)}
    factors = {'L0_ffn_bias': 4.778, 'L0_ffn_coeffs': 2.712}
    for name, (base, spread) in spreads.items():
        noise = np.random.default_rng([zlib.crc32(name.encode()), seed]).standard_normal(out[name].shape)
        drawn = base * np.exp(spread * noise) if base else spread * noise
        out[name] = jnp.asarray(drawn.astype(out[name].dtype))
    for name, factor in factors.items():
        out[name] = (out[name] * factor).astype(out[name].dtype)
    return out
```

```python
from contextlib import ExitStack

import numpy as np

import concourse.bass as bass
from concourse import mybir

F32 = mybir.dt.float32
F16 = mybir.dt.float16
I32 = mybir.dt.int32
ALU = mybir.AluOpType
ACT = mybir.ActivationFunctionType
AX = mybir.AxisListType

T = 128
BATCH, L, D = 8, 512, 2048
TB = L // T
CH = 512
CHUNKS = D // CH
N = BATCH * CHUNKS
SUB = CH // T
TOPK = int(2 * np.log(L))
KEPT2 = TOPK - 8
NEG = -3.0e38
EPS = 1e-5
ROWS = BATCH * L
TILES = ROWS // T
OT = D // T
DB = D // T
EXPERTS, RANK = 16, 16
ER = EXPERTS * RANK // T
W_SCALE = 2.0 ** 14
H_SCALE = 2.0 ** 10
ROOT2 = float(np.sqrt(2.0))
EXP_BITS = 0x7F800000
INV_BITS = 0x7F000000


def transform_matrices():
    m = np.arange(T)
    half, t = np.arange(2 * T), np.arange(L)
    plus = half[(half % 4 == 0) | (half % 4 == 3)]
    minus = half[(half % 4 == 1) | (half % 4 == 2)]
    omegas = [2 * np.pi * 2 * m / L, 2 * np.pi * (2 * m + 1) / L,
              np.pi * (2 * plus + 1) / L, np.pi * (2 * minus + 1) / L]

    def waves(omega, at):
        return np.stack([np.cos(np.outer(at, omega)), np.sin(np.outer(at, omega))])

    fwd = np.stack([waves(w, half) for w in omegas])
    fwd[0, 1, :, 0] = np.cos(np.pi * half)
    fwd = fwd.reshape(4, 2, 2, T, T).transpose(3, 0, 1, 2, 4)

    padded = np.zeros((2, 2, 4, T, T))
    for c, sign in enumerate((1.0, -1.0)):
        wave = waves(omegas[2 + c], t)
        padded[c, :, 0] = wave[:, :T]
        padded[c, :, 1] = wave[:, T:2 * T]
        padded[c, :, 2] = -sign * np.sqrt(2) * wave[:, :T]
        padded[c, :, 3] = sign * np.sqrt(2) * wave[:, T:2 * T]
        padded[c, :, 2, T - 1] -= wave.sum(1)
    padded = padded.transpose(3, 0, 1, 2, 4)
    tail = np.zeros((T, T))
    tail[T - 1, 0] = L

    inv = np.stack([2 * waves(w, half).transpose(0, 2, 1) / L for w in omegas[:2]])
    inv[0, 0, 0] /= 2
    inv[0, 1, 0] = np.cos(np.pi * half) / L
    inv = inv.transpose(2, 0, 1, 3)

    full = np.stack([waves(w, t).transpose(0, 2, 1) / L for w in omegas])
    full[:, 1] *= -1
    full[0, 0, 0] /= 2
    full[0, 1, 0] = np.cos(np.pi * t) / (2 * L)
    near = ((full[..., :2 * T] + full[..., 2 * T:]) / 2)[[0, 2, 3]]
    far = ((full[..., :2 * T] - full[..., 2 * T:]) / 2)[[1, 2, 3]]
    out = np.stack([near, far]).reshape(2, 3, 2, T, 2, T).transpose(3, 0, 4, 1, 2, 5)

    return {"fwd": fwd, "padded": padded, "tail": tail, "inv": inv, "out": out, "ident": np.eye(T)}


def at_least(engine, sem, value):
    if isinstance(value, int) and value <= 0:
        return
    engine.wait_ge(sem, value)


def wait_apart(nc, engine, sem, value, cell):
    at_least(engine, sem, value)
    nc.vector.memset(cell, 0.0)


def prepare(nc, x, W, A, Bf, coeffs, scales, ident, stat, whi, wlo, wscale):
    x_rows = x.rearrange("b l d -> (b l) d")
    with ExitStack() as ctx:
        sb = lambda name, shape, dt=F32: ctx.enter_context(nc.sbuf_tensor(name, shape, dt))
        sem = lambda name: ctx.enter_context(nc.semaphore(name))
        ident_sb = sb("p_ident", [T, T])
        a_sb = sb("p_a", [T, ER, D])
        mix = sb("p_mix", [T, ER])
        mix2 = sb("p_mix2", [T, ER])
        w_sb = [sb(f"p_w{i}", [T, D]) for i in range(2)]
        b_sb = [sb(f"p_b{i}", [T, EXPERTS, RANK]) for i in range(2)]
        bt_sb = [sb(f"p_bt{i}", [T, ER, T]) for i in range(2)]
        hi_sb = [sb(f"p_hi{i}", [T, DB, T], F16) for i in range(2)]
        lo_sb = [sb(f"p_lo{i}", [T, DB, T], F16) for i in range(2)]
        x_sb = [sb(f"p_x{i}", [T, D]) for i in range(2)]
        bn = [sb(f"p_bn{i}", [T, 4, 6]) for i in range(2)]
        idle = sb("p_idle", [1, 1])
        mv1 = sb("p_mv1", [T, 2])
        mv = sb("p_mv", [T, TILES, 2])
        largest = sb("p_largest", [T, 1])
        floor2 = sb("p_floor2", [T, 1])
        inverse2 = sb("p_inverse2", [T, 1])
        up = [sb(f"p_up{i}", [T, 1]) for i in range(2)]
        down = [sb(f"p_down{i}", [T, 1]) for i in range(2)]
        root = sb("p_root", [T, TILES])
        veps = sb("p_veps", [T, TILES])
        r0 = sb("p_r0", [T, TILES])
        sq = sb("p_sq", [T, TILES])
        delta_ps = ctx.enter_context(nc.psum_tensor("p_delta", [T, D], F32))
        t_ps = ctx.enter_context(nc.psum_tensor("p_t", [T, DB, T], F32))

        const_in = sem("p_const_in")
        w_in = [sem(f"p_w_in{i}") for i in range(2)]
        b_in = [sem(f"p_b_in{i}") for i in range(2)]
        x_in = [sem(f"p_x_in{i}") for i in range(2)]
        stored = [sem(f"p_stored{i}") for i in range(2)]
        mixed = sem("p_mixed")
        b_turned = sem("p_b_turned")
        b_weighted = sem("p_b_weighted")
        delta_mm = sem("p_delta_mm")
        w_added = sem("p_w_added")
        w_scale_known = sem("p_w_scale_known")
        w_scaled = sem("p_w_scaled")
        w_turned = sem("p_w_turned")
        hi_done = sem("p_hi_done")
        lo_done = sem("p_lo_done")
        link = sem("p_link")
        x_read = sem("p_x_read")
        row_done = sem("p_row_done")
        row_copied = sem("p_row_copied")
        var_done = sem("p_var_done")
        root_done = sem("p_root_done")
        block = ctx.enter_context(nc.Block())

        @block.sync
        def _(sp):
            sp.dma_start(ident_sb[:, :], ident).then_inc(const_in, 16)
            sp.dma_start(a_sb[:, :, :], A.rearrange("(h e) r d -> (e r) h d", h=ER)).then_inc(const_in, 16)
            per = EXPERTS // ER
            for h in range(ER):
                for vec, dst in ((coeffs, mix), (scales, mix2)):
                    part = vec[h * per:(h + 1) * per].unsqueeze(1).broadcast_to([per, RANK])
                    sp.dma_start(dst[:, h:h + 1], part.unsqueeze(2)).then_inc(const_in, 16)

            def load(b, c):
                n = 2 * b + c
                p = c % 2
                if not (isinstance(n, int) and n < 2):
                    at_least(sp, w_turned, n - 1)
                sp.dma_start(w_sb[p][:, :], W[bass.ts(n, T), :]).then_inc(w_in[p], 16)
                sp.dma_start(b_sb[p][:, :, :], Bf[:, bass.ts(n, T), :].rearrange("e o r -> o e r")
                             ).then_inc(b_in[p], 16)
                for i in range(2):
                    at_least(sp, x_read, 2 * n + i - 1)
                    sp.dma_start(x_sb[i][:, :], x_rows[bass.ts(2 * n + i, T), :]).then_inc(x_in[i], 16)

            def store(b, c):
                n = 2 * b + c
                p = c % 2
                sp.wait_ge(lo_done, n + 1)
                sp.wait_ge(hi_done, n + 1)
                sp.wait_ge(w_scale_known, n + 1)
                sp.dma_start(whi[:, bass.ds(n, 1)].rearrange("p a k o -> p (a k o)"),
                             hi_sb[p][:, :, :].rearrange("p k o -> p (k o)")).then_inc(stored[p], 16)
                sp.dma_start(wlo[:, bass.ds(n, 1)].rearrange("p a k o -> p (a k o)"),
                             lo_sb[p][:, :, :].rearrange("p k o -> p (k o)")).then_inc(stored[p], 16)
                sp.dma_start(wscale[bass.ts(n, T)].unsqueeze(1), down[p][:, :]).then_inc(stored[p], 16)

            load(0, 0)
            load(0, 1)
            store(0, 0)
            load(0, 2)
            with sp.Fori(0, OT // 2 - 2) as b:
                for c in range(1, 3):
                    store(b, c)
                    load(b, c + 2)
            for c in range(1, 4):
                store(OT // 2 - 2, c)
                if c == 1:
                    load(OT // 2 - 2, 3)
            for p in range(2):
                sp.wait_ge(stored[p], 48 * (OT // 2))

        @block.tensor
        def _(pe):
            def weights(b, c):
                n = 2 * b + c
                p = c % 2
                pe.wait_ge(b_in[p], 16 * (b + c // 2 + 1))
                at_least(pe, lo_done, n - 1)
                flat = b_sb[p][:, :, :].rearrange("o e r -> o (e r)")
                for h in range(ER):
                    last = nc.tensor.transpose(t_ps[:, h, :], flat[:, h * T:(h + 1) * T], ident_sb[:, :])
                last.then_inc(b_turned, 1)
                pe.wait_ge(b_weighted, n + 1)
                at_least(pe, w_added, n)
                for j in range(D // CH):
                    for h in range(ER):
                        last = nc.tensor.matmul(delta_ps[:, j * CH:(j + 1) * CH], bt_sb[p][:, h, :],
                                                a_sb[:, h, j * CH:(j + 1) * CH],
                                                start=(h == 0), stop=(h == ER - 1))
                last.then_inc(delta_mm, 1)

            def turn(b, c):
                n = 2 * b + c
                p = c % 2
                pe.wait_ge(w_scaled, n + 1)
                if not (isinstance(n, int) and n == OT - 1):
                    pe.wait_ge(b_weighted, n + 2)
                for k in range(DB):
                    last = nc.tensor.transpose(t_ps[:, k, :], w_sb[p][:, k * T:(k + 1) * T], ident_sb[:, :])
                last.then_inc(w_turned, 1)

            pe.wait_ge(const_in, 32 + 32 * ER)
            weights(0, 0)
            weights(0, 1)
            turn(0, 0)
            with pe.Fori(0, OT // 2 - 1) as b:
                for c in range(1, 3):
                    weights(b, c + 1)
                    turn(b, c)
            turn(OT // 2 - 1, 1)

        @block.scalar
        def _(act):
            def weigh(b, c):
                n = 2 * b + c
                p = c % 2
                act.wait_ge(b_turned, n + 1)
                at_least(act, delta_mm, n - 1)
                for h in range(ER):
                    last = nc.scalar.activation(bt_sb[p][:, h, :], t_ps[:, h, :], ACT.Copy, scale=mix[:, h:h + 1])
                last.then_inc(b_weighted, 1)

            def split(b, c):
                n = 2 * b + c
                p = c % 2
                act.wait_ge(w_scale_known, n + 1)
                nc.scalar.activation(w_sb[p][:, :], w_sb[p][:, :], ACT.Copy, scale=up[p][:, 0:1]
                                     ).then_inc(w_scaled, 1)
                act.wait_ge(w_turned, n + 1)
                at_least(act, stored[p], 48 * (b + c // 2))
                nc.scalar.activation(hi_sb[p][:, :, :], t_ps[:, :, :], ACT.Copy).then_inc(hi_done, 1)

            act.wait_ge(mixed, 1)
            weigh(0, 0)
            for c in range(2):
                weigh(0, c + 1)
                split(0, c)
            with act.Fori(0, OT // 2 - 2) as b:
                for c in range(2, 4):
                    weigh(b, c + 1)
                    split(b, c)
            weigh(OT // 2 - 1, 1)
            split(OT // 2 - 1, 0)
            split(OT // 2 - 1, 1)
            act.wait_ge(var_done, 1)
            nc.scalar.activation(root[:, :], veps[:, :], ACT.Sqrt).then_inc(root_done, 1)

        @block.vector
        def _(dve):
            dve.wait_ge(const_in, 32 + 32 * ER)
            nc.vector.tensor_tensor(mix[:, :], mix[:, :], mix2[:, :], ALU.mult).then_inc(mixed, 1)
            LINKS = 4

            def tile(b, c):
                n = 2 * b + c
                p = c % 2
                dve.wait_ge(delta_mm, n + 1)
                dve.wait_ge(w_in[p], 16 * (b + c // 2 + 1))
                nc.vector.tensor_tensor(w_sb[p][:, :], w_sb[p][:, :], delta_ps[:, :], ALU.add).then_inc(w_added, 1)
                dve.wait_ge(w_added, n + 1)
                nc.vector.tensor_reduce(largest[:, :], w_sb[p][:, :], AX.X, ALU.max,
                                        apply_absolute_value=True).then_inc(link, 1)
                dve.wait_ge(link, LINKS * n + 1)
                nc.vector.tensor_scalar(largest[:, :], largest[:, :], 2.0 ** -100, None, ALU.max).then_inc(link, 1)
                dve.wait_ge(link, LINKS * n + 2)
                nc.vector.tensor_scalar(floor2[:, :].bitcast(I32), largest[:, :].bitcast(I32), EXP_BITS, None,
                                        ALU.bitwise_and).then_inc(link, 1)
                dve.wait_ge(link, LINKS * n + 3)
                nc.vector.tensor_scalar(inverse2[:, :].bitcast(I32), floor2[:, :].bitcast(I32), -1.0,
                                        float(INV_BITS), ALU.mult, ALU.add).then_inc(link, 1)
                dve.wait_ge(link, LINKS * n + 4)
                at_least(dve, w_scaled, n - 1)
                at_least(dve, stored[p], 48 * (b + c // 2))
                nc.vector.tensor_scalar(down[p][:, :], floor2[:, :], 1.0 / (W_SCALE * H_SCALE), None, ALU.mult)
                nc.vector.tensor_scalar(up[p][:, :], inverse2[:, :], W_SCALE, None, ALU.mult
                                        ).then_inc(w_scale_known, 1)
                for i in range(2):
                    dve.wait_ge(x_in[i], 16 * (n + 1))
                    at_least(dve, x_read, 2 * n + i - 1)
                    for j in range(4):
                        last = nc.vector.bn_stats(bn[i][:, j, :], x_sb[i][:, j * CH:(j + 1) * CH])
                    last.then_inc(x_read, 1)
                    wait_apart(nc, dve, x_read, 2 * n + i + 1, idle[:, :])
                    nc.vector.bn_aggr(mv1[:, :], bn[i][:, :, :].rearrange("p a s -> p (a s)")).then_inc(row_done, 1)
                    dve.wait_ge(row_done, 2 * n + i + 1)
                    nc.vector.tensor_copy(mv[:, bass.ds(2 * n + i, 1), :].rearrange("p a s -> p (a s)"), mv1[:, :]
                                          ).then_inc(row_copied, 1)
                    dve.wait_ge(row_copied, 2 * n + i + 1)
                dve.wait_ge(hi_done, n + 1)
                nc.vector.tensor_tensor(lo_sb[p][:, :, :], t_ps[:, :, :], hi_sb[p][:, :, :], ALU.subtract
                                        ).then_inc(lo_done, 1)

            tile(0, 0)
            tile(0, 1)
            with dve.Fori(0, OT // 2 - 1) as b:
                for c in range(2, 4):
                    tile(b, c)
            dve.wait_ge(lo_done, OT)
            nc.vector.tensor_scalar(veps[:, :], mv[:, :, 1], EPS, None, ALU.add).then_inc(var_done, 1)
            dve.wait_ge(root_done, 1)
            k = LINKS * OT
            nc.vector.reciprocal(r0[:, :], root[:, :]).then_inc(link, 1)
            dve.wait_ge(link, k + 1)
            nc.vector.tensor_tensor(sq[:, :], r0[:, :], r0[:, :], ALU.mult).then_inc(link, 1)
            dve.wait_ge(link, k + 2)
            nc.vector.tensor_tensor(sq[:, :], sq[:, :], veps[:, :], ALU.mult).then_inc(link, 1)
            dve.wait_ge(link, k + 3)
            nc.vector.tensor_scalar(sq[:, :], sq[:, :], -0.5, 1.5, ALU.mult, ALU.add).then_inc(link, 1)
            dve.wait_ge(link, k + 4)
            nc.vector.tensor_tensor(stat[:, 0, :], r0[:, :], sq[:, :], ALU.mult).then_inc(link, 1)
            dve.wait_ge(link, k + 5)
            nc.vector.scalar_tensor_tensor(out=stat[:, 1, :], in0=mv[:, :, 0], scalar=-1.0, in1=stat[:, 0, :],
                                           op0=ALU.mult, op1=ALU.mult).then_inc(link, 1)
            dve.wait_ge(link, k + 6)


def attend(nc, x, values, consts, stat, x1):
    with ExitStack() as ctx:
        sb = lambda name, shape, dt=F32: ctx.enter_context(nc.sbuf_tensor(name, shape, dt))
        sem = lambda name: ctx.enter_context(nc.semaphore(name))
        fwd = sb("a_fwd", [T, 4, 2, 2, T])
        padded = sb("a_padded", [T, 2, 2, 4, T])
        tail = sb("a_tail", [T, T])
        inv = sb("a_inv", [T, 2, 2, 2 * T])
        outm = sb("a_out", [T, 2, 2, 3, 2, T])
        ident = sb("a_ident", [T, T])
        idle = sb("a_idle", [1, 2 * SUB + 2])
        idle_act = sb("a_idle_act", [T, 1])
        rows_but_0 = sb("a_rows_but_0", [T, 1])
        xs = [sb(f"a_x{i}", [T, TB, CH]) for i in range(4)]
        vs = [sb(f"a_v{i}", [T, TB, CH]) for i in range(2)]
        v_even = sb("a_v_even", [T, 2, CH])
        qs = sb("a_q", [T, TB, CH])
        q_even = sb("a_q_even", [T, 2, CH])
        vc = [sb(f"a_vc{i}", [T, 5, CH]) for i in range(2)]
        vn = [sb(f"a_vn{i}", [T, 4, CH]) for i in range(2)]
        prod = sb("a_prod", [T, 4, CH])
        term = sb("a_term", [T, 4, CH])
        zc = sb("a_zc", [T, 4, CH])
        zn = sb("a_zn", [T, 4, CH])
        corr = sb("a_corr", [T, SUB, L])
        wts = sb("a_wts", [T, SUB, L])
        side = sb("a_side", [T, 2, CH])
        w_high = sb("a_w_high", [T, 2, CH])
        w_even = sb("a_w_even", [T, 2, CH])
        w_odd = sb("a_w_odd", [T, 2, CH])
        w_quad = sb("a_w_quad", [T, 4, CH])
        top_a = sb("a_top_a", [T, SUB, 8])
        top_b = sb("a_top_b", [T, SUB, 8])
        minus_max = sb("a_minus_max", [T, SUB])
        total = sb("a_total", [T, SUB])
        share = sb("a_share", [T, SUB])
        ga = ctx.enter_context(nc.psum_tensor("a_ga", [T, 4, CH], F32))
        gb = ctx.enter_context(nc.psum_tensor("a_gb", [T, 4, CH], F32))

        const_in = sem("a_const_in")
        mask_set = sem("a_mask_set")
        x_in = [sem(f"a_x_in{i}") for i in range(4)]
        v_in = [sem(f"a_v_in{i}") for i in range(2)]
        x1_out = [sem(f"a_x1_out{i}") for i in range(4)]
        q_normed = sem("a_q_normed")
        vc_moved = sem("a_vc_moved")
        twin_copied = sem("a_twin_copied")
        high_moved = sem("a_high_moved")
        vn_moved = sem("a_vn_moved")
        odd_moved = sem("a_odd_moved")
        exp_done = sem("a_exp_done")
        weights_done = sem("a_weights_done")
        far_moved = sem("a_far_moved")
        q_summed = sem("a_q_summed")
        q_folded = sem("a_q_folded")
        v_summed = sem("a_v_summed")
        v_folded = sem("a_v_folded")
        prod_added = sem("a_prod_added")
        zc_added = sem("a_zc_added")
        zn_added = sem("a_zn_added")
        far_added = sem("a_far_added")
        v_cyc_mm = sem("a_v_cyc_mm")
        q_mm = sem("a_q_mm")
        turned = sem("a_turned")
        v_neg_mm = sem("a_v_neg_mm")
        w_cyc_mm = sem("a_w_cyc_mm")
        w_neg_mm = sem("a_w_neg_mm")
        corr_mm = sem("a_corr_mm")
        out_mm = sem("a_out_mm")
        prod_terms = sem("a_prod_terms")
        w_folded = sem("a_w_folded")
        w_quads = sem("a_w_quads")
        zc_terms = sem("a_zc_terms")
        zn_terms = sem("a_zn_terms")
        corr_folded = sem("a_corr_folded")
        top_a_found = sem("a_top_a_found")
        max_negated = sem("a_max_negated")
        first_marked = sem("a_first_marked")
        top_b_found = sem("a_top_b_found")
        top_b_cut = sem("a_top_b_cut")
        all_marked = sem("a_all_marked")
        kept = sem("a_kept")
        share_known = sem("a_share_known")
        x1_ready = sem("a_x1_ready")
        block = ctx.enter_context(nc.Block())

        def chunk_of(dram, b, c):
            row = dram[bass.ds(b + c // CHUNKS, 1)] if not isinstance(b, int) else dram[b + c // CHUNKS:b + c // CHUNKS + 1]
            col = (c % CHUNKS) * CH
            return row[:, :, col:col + CH].rearrange("a (k p) d -> p (a k) d", p=T)

        def run(engine, before, step):
            before()
            step(0, 0, True, False)
            step(0, 1, True, True)
            with engine.Fori(0, BATCH - 1) as b:
                for c in range(2, CHUNKS + 2):
                    step(b, c, True, True)
            for c in range(2, CHUNKS):
                step(BATCH - 1, c, True, True)
            step(BATCH - 1, CHUNKS, False, True)

        @block.sync
        def _(sp):
            def load(b, c):
                n = 4 * b + c
                if isinstance(n, int) and n >= N:
                    return
                at_least(sp, v_neg_mm, n - 1)
                at_least(sp, x1_out[c % 4], 16 * (b + c // 4))
                sp.dma_start(vs[c % 2][:, :, :], chunk_of(values, b, c)).then_inc(v_in[c % 2], 16)
                sp.dma_start(xs[c % 4][:, :, :], chunk_of(x, b, c)).then_inc(x_in[c % 4], 16)

            def before():
                load(0, 0)
                for name, dst in (("fwd", fwd), ("padded", padded), ("tail", tail), ("inv", inv),
                                  ("out", outm), ("ident", ident)):
                    sp.dma_start(dst[:], consts[name]).then_inc(const_in, 16)
                load(0, 1)

            def step(b, c, front, back):
                if front:
                    load(b, c + 2)
                if back:
                    sp.wait_ge(x1_ready, 4 * b + c)
                    sp.dma_start(chunk_of(x1, b, c - 1), xs[(c - 1) % 4][:, :, :]).then_inc(x1_out[(c - 1) % 4], 16)

            run(sp, before, step)
            for i in range(4):
                sp.wait_ge(x1_out[i], 16 * BATCH)

        @block.tensor
        def _(pe):
            def transform(group, cls, source, first_bank):
                for k in range(2):
                    for j in range(2):
                        last = nc.tensor.matmul(group[:, first_bank + 2 * k, :], fwd[:, cls, k, j, :], source[j],
                                                start=(j == 0), stop=(j == 1))
                return last

            def before():
                pe.wait_ge(const_in, 16 * 6)

            def step(b, c, front, back):
                n = 4 * b + c
                if front:
                    v = vs[c % 2]
                    pe.wait_ge(v_folded, n + 1)
                    at_least(pe, corr_folded, n)
                    for k in range(2):
                        for j in range(2):
                            nc.tensor.matmul(ga[:, 2 * k, :], fwd[:, 0, k, j, :], v_even[:, j, :],
                                             start=(j == 0), stop=(j == 1 and k == 1))
                        if k == 0:
                            nc.tensor.matmul(ga[:, 0, :], tail[:, :], v[:, 3, :], start=False, stop=True)
                    transform(ga, 1, [v[:, 0, :], v[:, 1, :]], 1).then_inc(v_cyc_mm, 1)
                    pe.wait_ge(q_folded, n + 1)
                    at_least(pe, x1_ready, n - 1)
                    at_least(pe, far_moved, n - 1)
                    transform(gb, 0, [q_even[:, 0, :], q_even[:, 1, :]], 0)
                    transform(gb, 1, [qs[:, 0, :], qs[:, 1, :]], 1).then_inc(q_mm, 1)
                if back:
                    pe.wait_ge(weights_done, n)
                    if front:
                        pe.wait_ge(vc_moved, n + 1)
                    else:
                        pe.wait_ge(corr_folded, n)
                    for k in range(TB):
                        for g in range(SUB):
                            last = nc.tensor.transpose(ga[:, k, g * T:(g + 1) * T], wts[:, g, k * T:(k + 1) * T],
                                                       ident[:, :])
                    last.then_inc(turned, 1)
                if front:
                    pe.wait_ge(prod_terms, n + 1)
                    blocks = [v[:, 0, :], v_even[:, 1, :], v[:, 3, :], v[:, 2, :]]
                    for cls in range(2):
                        for k in range(2):
                            for j in range(4):
                                last = nc.tensor.matmul(gb[:, 2 * k + cls, :], padded[:, cls, k, j, :], blocks[j],
                                                        start=(j == 0), stop=(j == 3))
                    last.then_inc(v_neg_mm, 1)
                if back:
                    pe.wait_ge(w_folded, n)
                    transform(ga, 0, [w_even[:, 0, :], w_even[:, 1, :]], 0)
                    transform(ga, 1, [w_odd[:, 0, :], w_odd[:, 1, :]], 1).then_inc(w_cyc_mm, 1)
                    pe.wait_ge(w_quads, n)
                    if front:
                        pe.wait_ge(vn_moved, n + 1)
                    else:
                        pe.wait_ge(x1_ready, n - 1)
                        pe.wait_ge(far_moved, n - 1)
                    for cls in range(2):
                        last = transform(gb, 2 + cls, [w_quad[:, 2 * cls, :], w_quad[:, 2 * cls + 1, :]], cls)
                    last.then_inc(w_neg_mm, 1)
                if front:
                    pe.wait_ge(prod_added, n + 1)
                    if back:
                        pe.wait_ge(zc_terms, n)
                    else:
                        pe.wait_ge(vc_moved, n + 1)
                    for g in range(SUB):
                        for cls in range(2):
                            for k in range(2):
                                last = nc.tensor.matmul(ga[:, g, cls * 2 * T:(cls + 1) * 2 * T],
                                                        prod[:, 2 * k + cls, g * T:(g + 1) * T],
                                                        inv[:, cls, k, :], start=(k == 0), stop=(k == 1))
                    last.then_inc(corr_mm, 1)
                if back:
                    pe.wait_ge(zc_added, n)
                    pe.wait_ge(zn_terms, n)
                    for half in range(2):
                        for j in range(2):
                            for k in range(2):
                                nc.tensor.matmul(gb[:, 2 * half + j, :], outm[:, half, j, 0, k, :],
                                                 zc[:, 2 * k + half, :], start=(k == 0), stop=False)
                    pe.wait_ge(zn_added, n)
                    for half in range(2):
                        for j in range(2):
                            for cls in range(2):
                                for k in range(2):
                                    last = nc.tensor.matmul(gb[:, 2 * half + j, :], outm[:, half, j, 1 + cls, k, :],
                                                            zn[:, 2 * k + cls, :], start=False,
                                                            stop=(cls == 1 and k == 1))
                    last.then_inc(out_mm, 1)

            run(pe, before, step)

        @block.scalar
        def _(act):
            def normalise(b, c):
                n = 4 * b + c
                if isinstance(n, int) and n >= N:
                    return
                act.wait_ge(x_in[c % 4], 16 * (b + c // 4 + 1))
                at_least(act, q_mm, n)
                nc.scalar.activation(idle_act[:, :], rows_but_0[:, :], ACT.Copy)
                for k in range(TB):
                    tile = 4 * (b + c // CHUNKS) + k
                    last = nc.scalar.activation(qs[:, k, :], xs[c % 4][:, k, :], ACT.Identity,
                                                bias=stat[:, 1, bass.ds(tile, 1)], scale=stat[:, 0, bass.ds(tile, 1)])
                last.then_inc(q_normed, 1)

            def before():
                act.wait_ge(mask_set, 2)
                normalise(0, 0)

            def step(b, c, front, back):
                n = 4 * b + c
                if front:
                    act.wait_ge(v_cyc_mm, n + 1)
                    at_least(act, zc_terms, n - 1)
                    dst = vc[c % 2]
                    nc.scalar.activation(dst[:, 4, :], ga[:, 0, :], ACT.Copy).then_inc(twin_copied, 1)
                    nc.scalar.activation(dst[:, 0:2, :], ga[:, 0:2, :], ACT.Copy)
                    nc.scalar.activation(dst[:, 2, :], ga[:, 2, :], ACT.Copy, scale=rows_but_0[:, 0:1])
                    nc.scalar.activation(dst[:, 3, :], ga[:, 3, :], ACT.Copy)
                    act.wait_ge(twin_copied, n + 1)
                    nc.scalar.activation(dst[0:1, 4, :], ga[0:1, 2, :], ACT.Copy).then_inc(vc_moved, 1)
                if back:
                    act.wait_ge(turned, n)
                    at_least(act, w_quads, n - 1)
                    nc.scalar.activation(w_high[:, :, :], ga[:, 2:4, :], ACT.Copy).then_inc(high_moved, 1)
                if front:
                    normalise(b, c + 1)
                    act.wait_ge(v_neg_mm, n + 1)
                    at_least(act, zn_terms, n - 1)
                    nc.scalar.activation(vn[c % 2][:, :, :], gb[:, :, :], ACT.Copy).then_inc(vn_moved, 1)
                    act.wait_ge(corr_mm, n + 1)
                    at_least(act, far_added, n - 1)
                    nc.scalar.activation(side[:, :, :].rearrange("p a (s l) -> p (a s) l", l=2 * T),
                                         ga[:, :, 2 * T:4 * T], ACT.Copy).then_inc(odd_moved, 1)
                    act.wait_ge(max_negated, n + 1)
                    at_least(act, turned, n)
                    for g in range(SUB):
                        nc.scalar.activation(wts[:, g, :], corr[:, g, :], ACT.Exp, bias=minus_max[:, g:g + 1]
                                             ).then_inc(exp_done, 1)
                    act.wait_ge(share_known, n + 1)
                    for g in range(SUB):
                        last = nc.scalar.activation(wts[:, g, :], wts[:, g, :], ACT.Copy, scale=share[:, g:g + 1])
                    last.then_inc(weights_done, 1)
                if back:
                    act.wait_ge(out_mm, n)
                    if front:
                        act.wait_ge(corr_folded, n + 1)
                    else:
                        act.wait_ge(far_added, n - 1)
                    nc.scalar.activation(side[:, :, :], gb[:, 2:4, :], ACT.Copy).then_inc(far_moved, 1)

            run(act, before, step)

        @block.gpsimd
        def _(pool):
            def fold(b, c):
                n = 4 * b + c
                if isinstance(n, int) and n >= N:
                    return
                v = vs[c % 2]
                pool.wait_ge(v_in[c % 2], 32 * b + 16 * (c // 2 + 1))
                at_least(pool, v_neg_mm, n)
                nc.gpsimd.tensor_tensor(v_even[:, :, :], v[:, 0:2, :], v[:, 2:4, :], ALU.add).then_inc(v_summed, 1)
                pool.wait_ge(v_summed, n + 1)
                nc.gpsimd.tensor_tensor(v[:, 0:2, :], v[:, 0:2, :], v[:, 2:4, :], ALU.subtract).then_inc(v_folded, 1)
                pool.wait_ge(q_normed, n + 1)
                nc.gpsimd.tensor_tensor(q_even[:, :, :], qs[:, 0:2, :], qs[:, 2:4, :], ALU.add).then_inc(q_summed, 1)
                pool.wait_ge(q_summed, n + 1)
                nc.gpsimd.tensor_tensor(qs[:, 0:2, :], qs[:, 0:2, :], qs[:, 2:4, :], ALU.subtract
                                        ).then_inc(q_folded, 1)

            def add_terms(terms_ready, added, count, spectrum):
                pool.wait_ge(terms_ready, count)
                nc.gpsimd.tensor_tensor(spectrum[:, 0:2, :], spectrum[:, 0:2, :], term[:, 0:2, :], ALU.add)
                nc.gpsimd.tensor_tensor(spectrum[:, 2:4, :], spectrum[:, 2:4, :], term[:, 2:4, :], ALU.subtract
                                        ).then_inc(added, 1)

            def before():
                nc.gpsimd.memset(rows_but_0[:, :], 1.0).then_inc(mask_set, 1)
                pool.wait_ge(mask_set, 1)
                nc.gpsimd.memset(rows_but_0[0:1, :], 0.0).then_inc(mask_set, 1)
                fold(0, 0)

            def step(b, c, front, back):
                n = 4 * b + c
                if front:
                    add_terms(prod_terms, prod_added, n + 1, prod)
                if back:
                    add_terms(zc_terms, zc_added, n, zc)
                if front:
                    fold(b, c + 1)
                if back:
                    add_terms(zn_terms, zn_added, n, zn)
                    xk = xs[(c - 1) % 4]
                    pool.wait_ge(far_moved, n)
                    nc.gpsimd.tensor_tensor(xk[:, 0:2, :], xk[:, 0:2, :], side[:, :, :], ALU.add)
                    nc.gpsimd.tensor_tensor(xk[:, 2:4, :], xk[:, 2:4, :], side[:, :, :], ALU.subtract
                                            ).then_inc(far_added, 1)

            run(pool, before, step)

        @block.vector
        def _(dve):
            def multiply(r, i, vr, vi, spectrum, twin):
                mul = lambda o, a, s: nc.vector.tensor_tensor(o, a, s, ALU.mult)
                mul(spectrum[:, 0:2, :], r, vr)
                mul(term[:, 0:2, :], i, vi)
                if twin is None:
                    mul(spectrum[:, 2:4, :], i, vr)
                else:
                    mul(spectrum[:, 2, :], i[:, 0, :], twin)
                    mul(spectrum[:, 3, :], i[:, 1, :], vr[:, 1, :])
                return mul(term[:, 2:4, :], r, vi)

            def choose(n):
                wait_apart(nc, dve, corr_folded, n + 1, idle[:, 0:1])
                for g in range(SUB):
                    last = nc.vector.max(top_a[:, g, :], corr[:, g, :])
                last.then_inc(top_a_found, 1)
                dve.wait_ge(top_a_found, n + 1)
                nc.vector.tensor_scalar(minus_max[:, :], top_a[:, :, 0], -1.0, None, ALU.mult).then_inc(max_negated, 1)
                for g in range(SUB):
                    wait_apart(nc, dve, exp_done, SUB * n + g + 1, idle[:, 1 + g:2 + g])
                    nc.vector.match_replace(corr[:, g, :], top_a[:, g, :], corr[:, g, :], NEG
                                            ).then_inc(first_marked, 1)
                for g in range(SUB):
                    wait_apart(nc, dve, first_marked, SUB * n + g + 1, idle[:, 1 + SUB + g:2 + SUB + g])
                    last = nc.vector.max(top_b[:, g, :], corr[:, g, :])
                last.then_inc(top_b_found, 1)
                dve.wait_ge(top_b_found, n + 1)
                nc.vector.memset(top_b[:, :, KEPT2:8], NEG).then_inc(top_b_cut, 1)
                wait_apart(nc, dve, top_b_cut, n + 1, idle[:, 1 + 2 * SUB:2 + 2 * SUB])
                for g in range(SUB):
                    nc.vector.match_replace(corr[:, g, :], top_b[:, g, :], corr[:, g, :], NEG
                                            ).then_inc(all_marked, 1)
                for g in range(SUB):
                    dve.wait_ge(all_marked, SUB * n + g + 1)
                    last = nc.vector.scalar_tensor_tensor(out=wts[:, g, :], in0=corr[:, g, :], scalar=NEG,
                                                          in1=wts[:, g, :], op0=ALU.is_le, op1=ALU.mult,
                                                          accum_out=total[:, g:g + 1])
                last.then_inc(kept, 1)
                dve.wait_ge(kept, n + 1)
                nc.vector.reciprocal(share[:, :], total[:, :]).then_inc(share_known, 1)

            def step(b, c, front, back):
                n = 4 * b + c
                if front:
                    vk = vc[c % 2]
                    dve.wait_ge(q_mm, n + 1)
                    dve.wait_ge(vc_moved, n + 1)
                    at_least(dve, corr_mm, n)
                    at_least(dve, zn_added, n - 1)
                    multiply(gb[:, 0:2, :], gb[:, 2:4, :], vk[:, 0:2, :], vk[:, 2:4, :], prod, vk[:, 4, :]
                             ).then_inc(prod_terms, 1)
                if back:
                    dve.wait_ge(high_moved, n)
                    at_least(dve, w_cyc_mm, n - 1)
                    nc.vector.tensor_tensor(w_even[:, :, :], ga[:, 0:2, :], w_high[:, :, :], ALU.add)
                    nc.vector.tensor_tensor(w_odd[:, :, :], ga[:, 0:2, :], w_high[:, :, :], ALU.subtract
                                            ).then_inc(w_folded, 1)
                    dve.wait_ge(w_folded, n)
                    at_least(dve, w_neg_mm, n - 1)
                    for cls, sign in enumerate((1.0, -1.0)):
                        nc.vector.scalar_tensor_tensor(out=w_quad[:, 2 * cls, :], in0=w_high[:, 1, :],
                                                       scalar=-sign * ROOT2, in1=w_odd[:, 0, :],
                                                       op0=ALU.mult, op1=ALU.add)
                        last = nc.vector.scalar_tensor_tensor(out=w_quad[:, 2 * cls + 1, :], in0=w_high[:, 0, :],
                                                              scalar=sign * ROOT2, in1=w_even[:, 1, :],
                                                              op0=ALU.mult, op1=ALU.add)
                    last.then_inc(w_quads, 1)
                    vk = vc[(c - 1) % 2]
                    dve.wait_ge(w_cyc_mm, n)
                    at_least(dve, out_mm, n - 1)
                    if front:
                        dve.wait_ge(prod_added, n + 1)
                    else:
                        dve.wait_ge(zn_added, n - 1)
                    multiply(ga[:, 0:2, :], ga[:, 2:4, :], vk[:, 0:2, :], vk[:, 2:4, :], zc, vk[:, 4, :]
                             ).then_inc(zc_terms, 1)
                    vk = vn[(c - 1) % 2]
                    dve.wait_ge(w_neg_mm, n)
                    dve.wait_ge(zc_added, n)
                    multiply(gb[:, 0:2, :], gb[:, 2:4, :], vk[:, 0:2, :], vk[:, 2:4, :], zn, None
                             ).then_inc(zn_terms, 1)
                if front:
                    dve.wait_ge(odd_moved, n + 1)
                    at_least(dve, kept, n)
                    odd = side[:, :, :].rearrange("p a (s l) -> p (a s) l", l=2 * T)
                    nc.vector.tensor_tensor(corr[:, :, 0:2 * T], ga[:, :, 0:2 * T], odd, ALU.add)
                    nc.vector.tensor_tensor(corr[:, :, 2 * T:L], ga[:, :, 0:2 * T], odd, ALU.subtract
                                            ).then_inc(corr_folded, 1)
                    choose(n)
                if back:
                    xk = xs[(c - 1) % 4]
                    dve.wait_ge(far_added, n)
                    nc.vector.tensor_tensor(xk[:, 0:2, :], gb[:, 0:2, :], xk[:, 0:2, :], ALU.add)
                    nc.vector.tensor_tensor(xk[:, 2:4, :], gb[:, 0:2, :], xk[:, 2:4, :], ALU.add
                                            ).then_inc(x1_ready, 1)

            run(dve, lambda: None, step)


def feed(nc, x1, bias, whi, wlo, wscale, ident, out):
    x_rows = x1.rearrange("b l d -> (b l) d")
    out_rows = out.rearrange("b l d -> (b l) d")
    G = 4
    OC = D // CH
    TG = CH // T
    with ExitStack() as ctx:
        sb = lambda name, shape, dt=F32: ctx.enter_context(nc.sbuf_tensor(name, shape, dt))
        sem = lambda name: ctx.enter_context(nc.semaphore(name))
        w_hi = sb("f_whi", [T, OT, DB, T], F16)
        w_lo = sb("f_wlo", [T, OT, DB, T], F16)
        ident_sb = sb("f_ident", [T, T])
        bias_sb = sb("f_bias", [T, D])
        scale_sb = sb("f_scale", [T, D])
        xs = [sb(f"f_x{i}", [T, D]) for i in range(G)]
        h = sb("f_h", [T, D])
        h_hi = [sb(f"f_hhi{i}", [T, DB, T], F16) for i in range(2)]
        h_lo = [sb(f"f_hlo{i}", [T, DB, T], F16) for i in range(2)]
        y = [sb(f"f_y{i}", [T, CH]) for i in range(2)]
        bn = sb("f_bn", [T, 4, 6])
        idle = sb("f_idle", [1, 1])
        mv = sb("f_mv", [T, 2])
        veps = sb("f_veps", [T, 1])
        root = sb("f_root", [T, 1])
        r0 = sb("f_r0", [T, 1])
        sq = sb("f_sq", [T, 1])
        gain = sb("f_gain", [T, 1])
        shift = sb("f_shift", [T, 1])
        out_ps = ctx.enter_context(nc.psum_tensor("f_out", [T, OC, CH], F32))
        t_ps = ctx.enter_context(nc.psum_tensor("f_t", [T, DB, T], F32))

        const_in = sem("f_const_in")
        w_in = [sem(f"f_w_in{i}") for i in range(OC)]
        x_in = [sem(f"f_x_in{i}") for i in range(G)]
        x_out = [sem(f"f_x_out{i}") for i in range(G)]
        link = sem("f_link")
        var_done = sem("f_var_done")
        root_done = sem("f_root_done")
        stats_done = sem("f_stats_done")
        h_done = sem("f_h_done")
        h_turned = sem("f_h_turned")
        hi_done = sem("f_hi_done")
        lo_done = sem("f_lo_done")
        out_mm = sem("f_out_mm")
        y_done = sem("f_y_done")
        bias_added = sem("f_bias_added")
        y_added = sem("f_y_added")
        block = ctx.enter_context(nc.Block())

        def run(engine, step):
            step(0, 0)
            step(0, 1)
            with engine.Fori(0, TILES // G - 1) as b:
                for c in range(2, G + 2):
                    step(b, c)
            for c in range(2, G):
                step(TILES // G - 1, c)

        @block.sync
        def _(sp):
            def load(b, c):
                n = G * b + c
                if isinstance(n, int) and n >= TILES:
                    return
                at_least(sp, x_out[c % G], 16 * (b + c // G))
                sp.dma_start(xs[c % G][:, :], x_rows[bass.ts(n, T), :]).then_inc(x_in[c % G], 16)

            def store(b, c):
                sp.wait_ge(y_added, OC * (G * b + c + 1))
                sp.dma_start(out_rows[bass.ts(G * b + c, T), :], xs[c % G][:, :]).then_inc(x_out[c % G], 16)

            load(0, 0)
            sp.dma_start(ident_sb[:, :], ident).then_inc(const_in, 16)
            for o in range(OC):
                part = slice(o * TG, (o + 1) * TG)
                sp.dma_start(w_hi[:, part], whi[:, part]).then_inc(w_in[o], 16)
                sp.dma_start(w_lo[:, part], wlo[:, part]).then_inc(w_in[o], 16)
                if o == 0:
                    sp.dma_start(bias_sb[:, :], bias.partition_broadcast(T)).then_inc(const_in, 16)
                    sp.dma_start(scale_sb[:, :], wscale.partition_broadcast(T)).then_inc(const_in, 16)
                    load(0, 1)
            load(0, 2)

            def step(b, c):
                load(b, c + 3)
                store(b, c)

            step(0, 0)
            with sp.Fori(0, TILES // G - 1) as b:
                for c in range(1, G + 1):
                    step(b, c)
            for c in range(1, G):
                step(TILES // G - 1, c)
            for i in range(G):
                sp.wait_ge(x_out[i], 16 * (TILES // G))

        @block.vector
        def _(dve):
            LINKS = 6

            def statistics(b, c):
                n = G * b + c
                if isinstance(n, int) and n >= TILES:
                    return
                dve.wait_ge(x_in[c % G], 16 * (b + c // G + 1))
                at_least(dve, h_done, n)
                for j in range(4):
                    last = nc.vector.bn_stats(bn[:, j, :], xs[c % G][:, j * CH:(j + 1) * CH])
                last.then_inc(link, 1)
                wait_apart(nc, dve, link, LINKS * n + 1, idle[:, :])
                nc.vector.bn_aggr(mv[:, :], bn[:, :, :].rearrange("p a s -> p (a s)")).then_inc(link, 1)
                dve.wait_ge(link, LINKS * n + 2)
                nc.vector.tensor_scalar(veps[:, :], mv[:, 1:2], EPS, None, ALU.add).then_inc(var_done, 1)
                dve.wait_ge(root_done, n + 1)
                nc.vector.reciprocal(r0[:, :], root[:, :]).then_inc(link, 1)
                dve.wait_ge(link, LINKS * n + 3)
                nc.vector.tensor_tensor(sq[:, :], r0[:, :], r0[:, :], ALU.mult).then_inc(link, 1)
                dve.wait_ge(link, LINKS * n + 4)
                nc.vector.tensor_tensor(sq[:, :], sq[:, :], veps[:, :], ALU.mult).then_inc(link, 1)
                dve.wait_ge(link, LINKS * n + 5)
                nc.vector.tensor_scalar(sq[:, :], sq[:, :], -0.5 * H_SCALE, 1.5 * H_SCALE, ALU.mult, ALU.add
                                        ).then_inc(link, 1)
                dve.wait_ge(link, LINKS * n + 6)
                nc.vector.tensor_tensor(gain[:, :], r0[:, :], sq[:, :], ALU.mult).then_inc(stats_done, 1)
                dve.wait_ge(stats_done, 2 * n + 1)
                nc.vector.scalar_tensor_tensor(out=shift[:, :], in0=mv[:, 0:1], scalar=-1.0, in1=gain[:, :],
                                               op0=ALU.mult, op1=ALU.mult).then_inc(stats_done, 1)

            def low(b, c):
                n = G * b + c
                if isinstance(n, int) and n >= TILES:
                    return
                dve.wait_ge(hi_done, n + 1)
                at_least(dve, out_mm, OC * (n - 1))
                nc.vector.tensor_tensor(h_lo[c % 2][:, :, :], t_ps[:, :, :], h_hi[c % 2][:, :, :], ALU.subtract
                                        ).then_inc(lo_done, 1)

            def rescale(b, c, o):
                n = G * b + c
                dve.wait_ge(out_mm, OC * n + o + 1)
                at_least(dve, y_added, OC * n + o - 1)
                nc.vector.tensor_tensor(y[o % 2][:, :], out_ps[:, o, :], scale_sb[:, o * CH:(o + 1) * CH], ALU.mult
                                        ).then_inc(y_done, 1)

            def step(b, c):
                rescale(b, c, 0)
                statistics(b, c + 2)
                rescale(b, c, 1)
                low(b, c + 1)
                rescale(b, c, 2)
                rescale(b, c, 3)

            dve.wait_ge(const_in, 48)
            statistics(0, 0)
            low(0, 0)
            statistics(0, 1)
            run(dve, step)

        @block.scalar
        def _(act):
            def take_root(b, c):
                n = G * b + c
                if isinstance(n, int) and n >= TILES:
                    return
                act.wait_ge(var_done, n + 1)
                nc.scalar.activation(root[:, :], veps[:, :], ACT.Sqrt).then_inc(root_done, 1)

            def normalise(b, c):
                n = G * b + c
                if isinstance(n, int) and n >= TILES:
                    return
                act.wait_ge(stats_done, 2 * n + 2)
                at_least(act, h_turned, n)
                nc.scalar.activation(h[:, :], xs[c % G][:, :], ACT.Identity, bias=shift[:, 0:1], scale=gain[:, 0:1]
                                     ).then_inc(h_done, 1)

            def high(b, c):
                n = G * b + c
                if isinstance(n, int) and n >= TILES:
                    return
                act.wait_ge(h_turned, n + 1)
                at_least(act, out_mm, OC * (n - 1))
                nc.scalar.activation(h_hi[c % 2][:, :, :], t_ps[:, :, :], ACT.Copy).then_inc(hi_done, 1)

            def step(b, c):
                take_root(b, c + 2)
                high(b, c + 1)
                normalise(b, c + 2)

            take_root(0, 0)
            normalise(0, 0)
            high(0, 0)
            take_root(0, 1)
            normalise(0, 1)
            run(act, step)

        @block.tensor
        def _(pe):
            def turn(b, c):
                n = G * b + c
                if isinstance(n, int) and n >= TILES:
                    return
                pe.wait_ge(h_done, n + 1)
                at_least(pe, lo_done, n)
                for k in range(DB):
                    last = nc.tensor.transpose(t_ps[:, k, :], h[:, k * T:(k + 1) * T], ident_sb[:, :])
                last.then_inc(h_turned, 1)

            def product(b, c, o):
                n = G * b + c
                at_least(pe, y_done, OC * (n - 1) + o + 1)
                part = slice(o * TG, (o + 1) * TG)
                for k in range(DB):
                    nc.tensor.matmul(out_ps[:, o, :], h_hi[c % 2][:, k, :], w_hi[:, part, k, :],
                                     start=(k == 0), stop=False)
                    nc.tensor.matmul(out_ps[:, o, :], h_hi[c % 2][:, k, :], w_lo[:, part, k, :],
                                     start=False, stop=False)
                    last = nc.tensor.matmul(out_ps[:, o, :], h_lo[c % 2][:, k, :], w_hi[:, part, k, :],
                                            start=False, stop=(k == DB - 1))
                last.then_inc(out_mm, 1)

            def step(b, c):
                n = G * b + c
                first = isinstance(n, int) and n == 0
                pe.wait_ge(lo_done, n + 1)
                for o in range(OC):
                    if o == 1:
                        turn(b, c + 1)
                    if first:
                        pe.wait_ge(w_in[o], 32)
                    product(b, c, o)

            pe.wait_ge(const_in, 48)
            turn(0, 0)
            run(pe, step)

        @block.gpsimd
        def _(pool):
            def add_bias(b, c):
                n = G * b + c
                if isinstance(n, int) and n >= TILES:
                    return
                pool.wait_ge(h_done, n + 1)
                nc.gpsimd.tensor_tensor(xs[c % G][:, :], xs[c % G][:, :], bias_sb[:, :], ALU.add
                                        ).then_inc(bias_added, 1)

            def step(b, c):
                n = G * b + c
                pool.wait_ge(bias_added, n + 1)
                for o in range(OC):
                    part = slice(o * CH, (o + 1) * CH)
                    pool.wait_ge(y_done, OC * n + o + 1)
                    nc.gpsimd.tensor_tensor(xs[c % G][:, part], xs[c % G][:, part], y[o % 2][:, :], ALU.add
                                            ).then_inc(y_added, 1)
                add_bias(b, c + 2)

            pool.wait_ge(const_in, 48)
            add_bias(0, 0)
            add_bias(0, 1)
            run(pool, step)


def program(nc, x, values, W, bias, A, Bf, coeffs, scales, consts, out):
    x1 = nc.dram_tensor("x1_scratch", [BATCH, L, D], F32, kind="Internal").ap()
    whi = nc.dram_tensor("whi_scratch", [T, OT, DB, T], F16, kind="Internal").ap()
    wlo = nc.dram_tensor("wlo_scratch", [T, OT, DB, T], F16, kind="Internal").ap()
    wscale = nc.dram_tensor("wscale_scratch", [D], F32, kind="Internal").ap()
    with nc.sbuf_tensor("stat", [T, 2, TILES], F32) as stat:
        prepare(nc, x, W, A, Bf, coeffs, scales, consts["ident"], stat, whi, wlo, wscale)
        attend(nc, x, values, consts, stat, x1)
        feed(nc, x1, bias, whi, wlo, wscale, consts["ident"], out)


_INS = ["x", "ctx_4096", "L0_ffn_W", "L0_ffn_bias", "L0_ffn_A", "L0_ffn_Bf", "L0_ffn_coeffs", "L0_ffn_scales"]


def kernel(**inputs):
    import concourse.bacc as _bacc
    from concourse.bass_utils import run_bass_kernel_spmd as _run

    nc = _bacc.Bacc("TRN2", target_bir_lowering=False, num_devices=1)
    arrays, args, consts = {}, [], {}
    for name in _INS:
        a = np.ascontiguousarray(inputs[name])
        arrays[f"in_{name}_dram"] = a
        args.append(nc.dram_tensor(f"in_{name}_dram", a.shape, mybir.dt.from_np(a.dtype), kind="ExternalInput").ap())
    for name, a in transform_matrices().items():
        a = np.ascontiguousarray(a.astype(np.float32))
        arrays[f"const_{name}_dram"] = a
        consts[name] = nc.dram_tensor(f"const_{name}_dram", a.shape, F32, kind="ExternalInput").ap()
    out = nc.dram_tensor("out_0_dram", (BATCH, L, D), F32, kind="ExternalOutput").ap()
    program(nc, *args, consts, out)
    r = _run(nc, [arrays], core_ids=[0])
    return r.results[0]["out_0_dram"]
```

```python
from contextlib import ExitStack

import numpy as np

import concourse.bass as bass
from concourse import mybir

F32 = mybir.dt.float32
F16 = mybir.dt.float16
I32 = mybir.dt.int32
ALU = mybir.AluOpType
ACT = mybir.ActivationFunctionType
AX = mybir.AxisListType

T = 128
BATCH, L, D = 8, 512, 2048
TB = L // T
CH = 512
CHUNKS = D // CH
N = BATCH * CHUNKS
SUB = CH // T
TOPK = int(2 * np.log(L))
KEPT2 = TOPK - 8
NEG = -3.0e38
EPS = 1e-5
ROWS = BATCH * L
TILES = ROWS // T
OT = D // T
DB = D // T
EXPERTS, RANK = 16, 16
ER = EXPERTS * RANK // T
W_SCALE = 2.0 ** 14
H_SCALE = 2.0 ** 10
ROOT2 = float(np.sqrt(2.0))
EXP_BITS = 0x7F800000
INV_BITS = 0x7F000000


def transform_matrices():
    m = np.arange(T)
    half, t = np.arange(2 * T), np.arange(L)
    plus = half[(half % 4 == 0) | (half % 4 == 3)]
    minus = half[(half % 4 == 1) | (half % 4 == 2)]
    omegas = [2 * np.pi * 2 * m / L, 2 * np.pi * (2 * m + 1) / L,
              np.pi * (2 * plus + 1) / L, np.pi * (2 * minus + 1) / L]

    def waves(omega, at):
        return np.stack([np.cos(np.outer(at, omega)), np.sin(np.outer(at, omega))])

    fwd = np.stack([waves(w, half) for w in omegas])
    fwd[0, 1, :, 0] = np.cos(np.pi * half)
    fwd = fwd.reshape(4, 2, 2, T, T).transpose(3, 0, 1, 2, 4)

    tail = np.zeros((T, T))
    tail[0, 0] = L

    inv = np.stack([2 * waves(w, half).transpose(0, 2, 1) / L for w in omegas[:2]])
    inv[0, 0, 0] /= 2
    inv[0, 1, 0] = np.cos(np.pi * half) / L
    inv = inv.transpose(2, 0, 1, 3)

    full = np.stack([waves(w, t).transpose(0, 2, 1) / L for w in omegas])
    full[:, 1] *= -1
    full[0, 0, 0] /= 2
    full[0, 1, 0] = np.cos(np.pi * t) / (2 * L)
    near = ((full[..., :2 * T] + full[..., 2 * T:]) / 2)[[0, 2, 3]]
    far = ((full[..., :2 * T] - full[..., 2 * T:]) / 2)[[1, 2, 3]]
    out = np.stack([near, far]).reshape(2, 3, 2, T, 2, T).transpose(3, 0, 4, 1, 2, 5)

    return {"fwd": fwd, "tail": tail, "inv": inv, "out": out, "ident": np.eye(T)}


def at_least(engine, sem, value):
    if isinstance(value, int) and value <= 0:
        return
    engine.wait_ge(sem, value)


def wait_apart(nc, engine, sem, value, cell):
    at_least(engine, sem, value)
    nc.vector.memset(cell, 0.0)


def inverse_root(nc, dve, act_root, veps, root, r0, sq, out, gain, link, base):
    act_root()
    nc.vector.reciprocal(r0, root).then_inc(link, 1)
    dve.wait_ge(link, base + 1)
    nc.vector.tensor_tensor(sq, r0, r0, ALU.mult).then_inc(link, 1)
    dve.wait_ge(link, base + 2)
    nc.vector.tensor_tensor(sq, sq, veps, ALU.mult).then_inc(link, 1)
    dve.wait_ge(link, base + 3)
    nc.vector.tensor_scalar(sq, sq, -0.5 * gain, 1.5 * gain, ALU.mult, ALU.add).then_inc(link, 1)
    dve.wait_ge(link, base + 4)
    return nc.vector.tensor_tensor(out, r0, sq, ALU.mult)


def prepare(nc, x, W, A, Bf, coeffs, scales, ident, stat, whi, wlo, wscale):
    x_rows = x.rearrange("b l d -> (b l) d")
    JC = D // CH
    with ExitStack() as ctx:
        sb = lambda name, shape, dt=F32: ctx.enter_context(nc.sbuf_tensor(name, shape, dt))
        sem = lambda name: ctx.enter_context(nc.semaphore(name))
        ident_sb = sb("p_ident", [T, T])
        a_sb = sb("p_a", [T, ER, D])
        mix = sb("p_mix", [T, ER])
        mix2 = sb("p_mix2", [T, ER])
        w_sb = [sb(f"p_w{i}", [T, D]) for i in range(4)]
        b_sb = [sb(f"p_b{i}", [T, EXPERTS, RANK]) for i in range(4)]
        bt_sb = [sb(f"p_bt{i}", [T, ER, T]) for i in range(2)]
        hi_sb = [sb(f"p_hi{i}", [T, DB, T], F16) for i in range(2)]
        lo_sb = [sb(f"p_lo{i}", [T, DB, T], F16) for i in range(2)]
        x_sb = [sb(f"p_x{i}", [T, D]) for i in range(TB)]
        bn = [sb(f"p_bn{i}", [T, 4, 6]) for i in range(TB)]
        mv = sb("p_mv", [T, TB, 2])
        largest = sb("p_largest", [T, 1])
        floor2 = sb("p_floor2", [T, 1])
        inverse2 = sb("p_inverse2", [T, 1])
        up = [sb(f"p_up{i}", [T, 1]) for i in range(2)]
        down = [sb(f"p_down{i}", [T, 1]) for i in range(2)]
        root = sb("p_root", [T, TB])
        veps = sb("p_veps", [T, TB])
        r0 = sb("p_r0", [T, TB])
        sq = sb("p_sq", [T, TB])
        b_ps = ctx.enter_context(nc.psum_tensor("p_b_ps", [T, TB, T], F32))
        delta_ps = ctx.enter_context(nc.psum_tensor("p_delta", [T, 2, CH], F32))
        t_ps = ctx.enter_context(nc.psum_tensor("p_t", [T, DB, T], F32))

        const_in = sem("p_const_in")
        w_in = [sem(f"p_w_in{i}") for i in range(4)]
        b_in = [sem(f"p_b_in{i}") for i in range(4)]
        x_in = [sem(f"p_x_in{i}") for i in range(TB)]
        stored = [sem(f"p_stored{i}") for i in range(2)]
        mixed = sem("p_mixed")
        b_turned = sem("p_b_turned")
        b_weighted = sem("p_b_weighted")
        delta_mm = sem("p_delta_mm")
        w_added = sem("p_w_added")
        w_scale_known = sem("p_w_scale_known")
        w_scaled = sem("p_w_scaled")
        w_turned = sem("p_w_turned")
        hi_done = sem("p_hi_done")
        lo_done = sem("p_lo_done")
        link = sem("p_link")
        rows_read = sem("p_rows_read")
        rows_done = sem("p_rows_done")
        var_done = sem("p_var_done")
        root_done = sem("p_root_done")
        block = ctx.enter_context(nc.Block())

        def run(engine, step):
            step(0, 0)
            step(0, 1)
            with engine.Fori(0, OT // 4 - 1) as b:
                for c in range(2, 6):
                    step(b, c)
            for c in range(2, 4):
                step(OT // 4 - 1, c)

        @block.sync
        def _(sp):
            def load(b, c):
                n = 4 * b + c
                p, q = c % 2, c % 4
                at_least(sp, w_turned, n - 3)
                sp.dma_start(b_sb[q][:, :, :], Bf[:, bass.ts(n, T), :].rearrange("e o r -> o e r")
                             ).then_inc(b_in[q], 16)
                sp.dma_start(w_sb[q][:, :], W[bass.ts(n, T), :]).then_inc(w_in[q], 16)

            def store(b, c):
                n = 4 * b + c
                p, q = c % 2, c % 4
                sp.wait_ge(lo_done, n + 1)
                sp.wait_ge(hi_done, n + 1)
                sp.wait_ge(w_scale_known, n + 1)
                sp.dma_start(whi[:, bass.ds(n, 1)].rearrange("p a k o -> p (a k o)"),
                             hi_sb[p][:, :, :].rearrange("p k o -> p (k o)")).then_inc(stored[p], 16)
                sp.dma_start(wlo[:, bass.ds(n, 1)].rearrange("p a k o -> p (a k o)"),
                             lo_sb[p][:, :, :].rearrange("p k o -> p (k o)")).then_inc(stored[p], 16)
                sp.dma_start(wscale[bass.ts(n, T)].unsqueeze(1), down[p][:, :]).then_inc(stored[p], 16)

            sp.dma_start(ident_sb[:, :], ident).then_inc(const_in, 16)
            per = EXPERTS // ER
            for h in range(ER):
                for vec, dst in ((coeffs, mix), (scales, mix2)):
                    part = vec[h * per:(h + 1) * per].unsqueeze(1).broadcast_to([per, RANK])
                    sp.dma_start(dst[:, h:h + 1], part.unsqueeze(2)).then_inc(const_in, 16)
            sp.dma_start(a_sb[:, :, :], A.rearrange("(h e) r d -> (e r) h d", h=ER)).then_inc(const_in, 16)
            load(0, 0)
            load(0, 1)
            for k in range(TB):
                sp.dma_start(x_sb[k][:, :], x_rows[k * T:(k + 1) * T, :]).then_inc(x_in[k], 16)

            def step(b, c):
                if not (isinstance(b, int) and 4 * b + c + 2 >= OT):
                    load(b, c + 2)
                store(b, c)

            run(sp, step)
            for p in range(2):
                sp.wait_ge(stored[p], 48 * (OT // 2))

        @block.tensor
        def _(pe):
            def weights(b, c):
                n = 4 * b + c
                p, q = c % 2, c % 4
                pe.wait_ge(b_in[q], 16 * (b + c // 4 + 1))
                at_least(pe, b_weighted, n)
                flat = b_sb[q][:, :, :].rearrange("o e r -> o (e r)")
                for h in range(ER):
                    last = nc.tensor.transpose(b_ps[:, h, :], flat[:, h * T:(h + 1) * T], ident_sb[:, :])
                last.then_inc(b_turned, 1)
                pe.wait_ge(b_weighted, n + 1)
                for j in range(JC):
                    at_least(pe, w_added, JC * n + j - 1)
                    for h in range(ER):
                        last = nc.tensor.matmul(delta_ps[:, j % 2, :], bt_sb[p][:, h, :],
                                                a_sb[:, h, j * CH:(j + 1) * CH],
                                                start=(h == 0), stop=(h == ER - 1))
                    last.then_inc(delta_mm, 1)

            def turn(b, c):
                n = 4 * b + c
                p, q = c % 2, c % 4
                pe.wait_ge(w_scaled, n + 1)
                at_least(pe, lo_done, n)
                for k in range(DB):
                    last = nc.tensor.transpose(t_ps[:, k, :], w_sb[q][:, k * T:(k + 1) * T], ident_sb[:, :])
                last.then_inc(w_turned, 1)

            pe.wait_ge(const_in, 32 + 32 * ER)
            weights(0, 0)

            def step(b, c):
                if not (isinstance(b, int) and 4 * b + c + 1 >= OT):
                    weights(b, c + 1)
                turn(b, c)

            run(pe, step)

        @block.scalar
        def _(act):
            def weigh(b, c):
                n = 4 * b + c
                p, q = c % 2, c % 4
                act.wait_ge(b_turned, n + 1)
                at_least(act, delta_mm, JC * (n - 1))
                for h in range(ER):
                    last = nc.scalar.activation(bt_sb[p][:, h, :], b_ps[:, h, :], ACT.Copy, scale=mix[:, h:h + 1])
                last.then_inc(b_weighted, 1)

            def split(b, c):
                n = 4 * b + c
                p, q = c % 2, c % 4
                act.wait_ge(w_scale_known, n + 1)
                nc.scalar.activation(w_sb[q][:, :], w_sb[q][:, :], ACT.Copy, scale=up[p][:, 0:1]
                                     ).then_inc(w_scaled, 1)
                act.wait_ge(w_turned, n + 1)
                at_least(act, stored[p], 48 * (2 * b + c // 2))
                nc.scalar.activation(hi_sb[p][:, :, :], t_ps[:, :, :], ACT.Copy).then_inc(hi_done, 1)

            act.wait_ge(mixed, 1)
            weigh(0, 0)
            act.wait_ge(var_done, 1)
            nc.scalar.activation(root[:, :], veps[:, :], ACT.Sqrt).then_inc(root_done, 1)

            def step(b, c):
                if not (isinstance(b, int) and 4 * b + c + 1 >= OT):
                    weigh(b, c + 1)
                split(b, c)

            run(act, step)

        @block.vector
        def _(dve):
            LINKS = 4

            def scale(b, c):
                n = 4 * b + c
                p, q = c % 2, c % 4
                dve.wait_ge(w_in[q], 16 * (b + c // 4 + 1))
                for j in range(JC):
                    dve.wait_ge(delta_mm, JC * n + j + 1)
                    part = w_sb[q][:, j * CH:(j + 1) * CH]
                    nc.vector.tensor_tensor(part, part, delta_ps[:, j % 2, :], ALU.add).then_inc(w_added, 1)
                dve.wait_ge(w_added, JC * n + JC)
                nc.vector.tensor_reduce(largest[:, :], w_sb[q][:, :], AX.X, ALU.max,
                                        apply_absolute_value=True).then_inc(link, 1)
                dve.wait_ge(link, LINKS * n + 1)
                nc.vector.tensor_scalar(largest[:, :], largest[:, :], 2.0 ** -100, None, ALU.max).then_inc(link, 1)
                dve.wait_ge(link, LINKS * n + 2)
                nc.vector.tensor_scalar(floor2[:, :].bitcast(I32), largest[:, :].bitcast(I32), EXP_BITS, None,
                                        ALU.bitwise_and).then_inc(link, 1)
                dve.wait_ge(link, LINKS * n + 3)
                nc.vector.tensor_scalar(inverse2[:, :].bitcast(I32), floor2[:, :].bitcast(I32), -1.0,
                                        float(INV_BITS), ALU.mult, ALU.add).then_inc(link, 1)
                dve.wait_ge(link, LINKS * n + 4)
                at_least(dve, w_scaled, n - 1)
                at_least(dve, stored[p], 48 * (2 * b + c // 2))
                nc.vector.tensor_scalar(down[p][:, :], floor2[:, :], 1.0 / (W_SCALE * H_SCALE), None, ALU.mult)
                nc.vector.tensor_scalar(up[p][:, :], inverse2[:, :], W_SCALE, None, ALU.mult
                                        ).then_inc(w_scale_known, 1)

            def low(b, c):
                n = 4 * b + c
                p, q = c % 2, c % 4
                dve.wait_ge(hi_done, n + 1)
                at_least(dve, stored[p], 48 * (2 * b + c // 2))
                nc.vector.tensor_tensor(lo_sb[p][:, :, :], t_ps[:, :, :], hi_sb[p][:, :, :], ALU.subtract
                                        ).then_inc(lo_done, 1)

            dve.wait_ge(const_in, 32 + 32 * ER)
            nc.vector.tensor_tensor(mix[:, :], mix[:, :], mix2[:, :], ALU.mult).then_inc(mixed, 1)
            for k in range(TB):
                dve.wait_ge(x_in[k], 16)
                for j in range(4):
                    last = nc.vector.bn_stats(bn[k][:, j, :], x_sb[k][:, j * CH:(j + 1) * CH])
            last.then_inc(rows_read, 1)
            dve.wait_ge(rows_read, 1)
            for k in range(TB):
                last = nc.vector.bn_aggr(mv[:, k, :], bn[k][:, :, :].rearrange("p a s -> p (a s)"))
            last.then_inc(rows_done, 1)
            dve.wait_ge(rows_done, 1)
            nc.vector.tensor_scalar(veps[:, :], mv[:, :, 1], EPS, None, ALU.add).then_inc(var_done, 1)

            def step(b, c):
                scale(b, c)
                if not (isinstance(b, int) and 4 * b + c == 0):
                    low(b, c - 1)

            run(dve, step)
            low(OT // 4 - 1, 3)
            k = LINKS * OT
            inverse_root(nc, dve, lambda: dve.wait_ge(root_done, 1), veps[:, :], root[:, :], r0[:, :], sq[:, :],
                         stat[:, 0, :], 1.0, link, k).then_inc(link, 1)
            dve.wait_ge(link, k + 5)
            nc.vector.scalar_tensor_tensor(out=stat[:, 1, :], in0=mv[:, :, 0], scalar=-1.0, in1=stat[:, 0, :],
                                           op0=ALU.mult, op1=ALU.mult).then_inc(link, 1)
            dve.wait_ge(link, k + 6)


def attend(nc, x, values, consts, stat, x1):
    x_rows = x.rearrange("b l d -> (b l) d")
    with ExitStack() as ctx:
        sb = lambda name, shape, dt=F32: ctx.enter_context(nc.sbuf_tensor(name, shape, dt))
        sem = lambda name: ctx.enter_context(nc.semaphore(name))
        fwd = sb("a_fwd", [T, 4, 2, 2, T])
        tail = sb("a_tail", [T, T])
        inv = sb("a_inv", [T, 2, 2, 2 * T])
        outm = sb("a_out", [T, 2, 2, 3, 2, T])
        ident = sb("a_ident", [T, T])
        idle = sb("a_idle", [1, 2 * SUB + 3])
        rows_but_0 = sb("a_rows_but_0", [T, 1])
        xs = [sb(f"a_x{i}", [T, TB, CH]) for i in range(4)]
        vs = [sb(f"a_v{i}", [T, TB, CH]) for i in range(2)]
        last = [sb(f"a_last{i}", [T, CH]) for i in range(2)]
        rows = sb("a_rows", [T, D])
        bn = sb("a_bn", [T, 4, 6])
        mv = sb("a_mv", [T, TB, 2])
        veps, root, r0, sq = (sb(f"a_{name}", [T, TB]) for name in ("veps", "root", "r0", "sq"))
        v_even = sb("a_v_even", [T, 2, CH])
        qs = sb("a_q", [T, TB, CH])
        q_even = sb("a_q_even", [T, 2, CH])
        vc = [sb(f"a_vc{i}", [T, 5, CH]) for i in range(2)]
        vn = [sb(f"a_vn{i}", [T, 4, CH]) for i in range(2)]
        prod = sb("a_prod", [T, 4, CH])
        term = sb("a_term", [T, 4, CH])
        zc = sb("a_zc", [T, 4, CH])
        zn = sb("a_zn", [T, 4, CH])
        corr = sb("a_corr", [T, SUB, L])
        wts = sb("a_wts", [T, SUB, L])
        side = sb("a_side", [T, 2, CH])
        w_high = sb("a_w_high", [T, 2, CH])
        w_even = sb("a_w_even", [T, 2, CH])
        w_odd = sb("a_w_odd", [T, 2, CH])
        w_quad = sb("a_w_quad", [T, 4, CH])
        top_a = sb("a_top_a", [T, SUB, 8])
        top_b = sb("a_top_b", [T, SUB, 8])
        minus_max = sb("a_minus_max", [T, SUB])
        total = sb("a_total", [T, SUB])
        share = sb("a_share", [T, SUB])
        ga = ctx.enter_context(nc.psum_tensor("a_ga", [T, 4, CH], F32))
        gb = ctx.enter_context(nc.psum_tensor("a_gb", [T, 4, CH], F32))

        const_in = sem("a_const_in")
        mask_set = sem("a_mask_set")
        x_in = [sem(f"a_x_in{i}") for i in range(4)]
        v_in = [sem(f"a_v_in{i}") for i in range(2)]
        x1_out = [sem(f"a_x1_out{i}") for i in range(4)]
        q_normed = sem("a_q_normed")
        vc_moved = sem("a_vc_moved")
        twin_copied = sem("a_twin_copied")
        high_moved = sem("a_high_moved")
        vn_moved = sem("a_vn_moved")
        odd_moved = sem("a_odd_moved")
        exp_done = sem("a_exp_done")
        weights_done = sem("a_weights_done")
        far_moved = sem("a_far_moved")
        q_summed = sem("a_q_summed")
        q_folded = sem("a_q_folded")
        v_summed = sem("a_v_summed")
        v_folded = sem("a_v_folded")
        v_lowered = sem("a_v_lowered")
        prod_added = sem("a_prod_added")
        zc_added = sem("a_zc_added")
        zn_added = sem("a_zn_added")
        x1_ready = sem("a_x1_ready")
        v_cyc_mm = sem("a_v_cyc_mm")
        q_mm = sem("a_q_mm")
        turned = sem("a_turned")
        v_neg_mm = sem("a_v_neg_mm")
        w_cyc_mm = sem("a_w_cyc_mm")
        w_neg_mm = sem("a_w_neg_mm")
        corr_mm = sem("a_corr_mm")
        out_mm = sem("a_out_mm")
        prod_half = sem("a_prod_half")
        prod_terms = sem("a_prod_terms")
        near_added = sem("a_near_added")
        v_shifted = sem("a_v_shifted")
        v_plus = sem("a_v_plus")
        v_quads = sem("a_v_quads")
        rows_read = sem("a_rows_read")
        rows_done = sem("a_rows_done")
        var_done = sem("a_var_done")
        root_link = sem("a_root_link")
        gain_done = sem("a_gain_done")
        stat_done = sem("a_stat_done")
        w_folded = sem("a_w_folded")
        w_quads = sem("a_w_quads")
        zc_terms = sem("a_zc_terms")
        zn_terms = sem("a_zn_terms")
        corr_folded = sem("a_corr_folded")
        top_a_found = sem("a_top_a_found")
        max_negated = sem("a_max_negated")
        first_marked = sem("a_first_marked")
        top_b_found = sem("a_top_b_found")
        top_b_cut = sem("a_top_b_cut")
        all_marked = sem("a_all_marked")
        kept = sem("a_kept")
        share_known = sem("a_share_known")
        rows_in = sem("a_rows_in")
        root_done = sem("a_root_done")
        block = ctx.enter_context(nc.Block())

        def chunk_of(dram, b, c):
            row = dram[bass.ds(b + c // CHUNKS, 1)] if not isinstance(b, int) else dram[b + c // CHUNKS:b + c // CHUNKS + 1]
            col = (c % CHUNKS) * CH
            return row[:, :, col:col + CH].rearrange("a (k p) d -> p (a k) d", p=T)

        def last_row_of(dram, b, c):
            row = dram[bass.ds(b + c // CHUNKS, 1)] if not isinstance(b, int) else dram[b + c // CHUNKS:b + c // CHUNKS + 1]
            col = (c % CHUNKS) * CH
            return row[:, L - 1, col:col + CH].rearrange("a d -> (a d)")

        def run(engine, before, step):
            before()
            step(0, 0, True, False)
            step(0, 1, True, True)
            with engine.Fori(0, BATCH - 2) as b:
                for c in range(2, CHUNKS + 2):
                    step(b, c, True, True)
            for c in range(2, 2 * CHUNKS):
                step(BATCH - 2, c, True, True)
            step(BATCH - 2, 2 * CHUNKS, False, True)

        @block.sync
        def _(sp):
            def load(b, c):
                n = 4 * b + c
                if isinstance(n, int) and n >= N:
                    return
                at_least(sp, v_neg_mm, n - 1)
                at_least(sp, x1_out[c % 4], 16 * (b + c // 4))
                sp.dma_start(vs[c % 2][:, :, :], chunk_of(values, b, c)).then_inc(v_in[c % 2], 16)
                sp.dma_start(last[c % 2][:, :], last_row_of(values, b, c).partition_broadcast(T)
                             ).then_inc(v_in[c % 2], 16)
                sp.dma_start(xs[c % 4][:, :, :], chunk_of(x, b, c)).then_inc(x_in[c % 4], 16)

            def before():
                load(0, 0)
                for name, dst in (("fwd", fwd), ("tail", tail), ("inv", inv),
                                  ("out", outm), ("ident", ident)):
                    sp.dma_start(dst[:], consts[name]).then_inc(const_in, 16)
                load(0, 1)

            def load_rows(b, c):
                n = 4 * b + c
                if isinstance(n, int) and n + TB >= TILES:
                    return
                at_least(sp, rows_read, n)
                sp.dma_start(rows[:, :], x_rows[bass.ts(n + TB, T), :]).then_inc(rows_in, 16)

            def step(b, c, front, back):
                if front:
                    load_rows(b, c)
                    load(b, c + 2)
                if back:
                    sp.wait_ge(x1_ready, 4 * b + c)
                    sp.dma_start(chunk_of(x1, b, c - 1), xs[(c - 1) % 4][:, :, :]).then_inc(x1_out[(c - 1) % 4], 16)

            run(sp, before, step)
            for i in range(4):
                sp.wait_ge(x1_out[i], 16 * BATCH)

        @block.tensor
        def _(pe):
            def transform(group, cls, source, first_bank):
                for k in range(2):
                    for j in range(2):
                        mm = nc.tensor.matmul(group[:, first_bank + 2 * k, :], fwd[:, cls, k, j, :], source[j],
                                                start=(j == 0), stop=(j == 1))
                return mm

            def before():
                pe.wait_ge(const_in, 16 * 5)

            def step(b, c, front, back):
                n = 4 * b + c
                if front:
                    v = vs[c % 2]
                    last_row = last[c % 2]
                    pe.wait_ge(v_folded, n + 1)
                    at_least(pe, corr_folded, n)
                    for k in range(2):
                        for j in range(2):
                            nc.tensor.matmul(ga[:, 2 * k, :], fwd[:, 0, k, j, :], v_even[:, j, :],
                                             start=(j == 0), stop=(j == 1 and k == 1))
                        if k == 0:
                            nc.tensor.matmul(ga[:, 0, :], tail[:, :], last_row[:, :], start=False, stop=True)
                    transform(ga, 1, [v[:, 0, :], v[:, 1, :]], 1).then_inc(v_cyc_mm, 1)
                    pe.wait_ge(q_folded, n + 1)
                    at_least(pe, near_added, n - 1)
                    at_least(pe, far_moved, n - 1)
                    transform(gb, 0, [q_even[:, 0, :], q_even[:, 1, :]], 0)
                    transform(gb, 1, [qs[:, 0, :], qs[:, 1, :]], 1).then_inc(q_mm, 1)
                if back:
                    pe.wait_ge(weights_done, n)
                    if front:
                        pe.wait_ge(vc_moved, n + 1)
                    else:
                        pe.wait_ge(corr_folded, n)
                    for k in range(TB):
                        for g in range(SUB):
                            mm = nc.tensor.transpose(ga[:, k, g * T:(g + 1) * T], wts[:, g, k * T:(k + 1) * T],
                                                       ident[:, :])
                    mm.then_inc(turned, 1)
                if front:
                    pe.wait_ge(v_quads, n + 1)
                    pe.wait_ge(prod_half, n + 1)
                    plus, minus = [v[:, 3, :], v[:, 2, :]], [v[:, 0, :], v_even[:, 1, :]]
                    for k in range(2):
                        if k == 1:
                            pe.wait_ge(prod_terms, n + 1)
                        for cls, source in enumerate((plus, minus)):
                            for j in range(2):
                                mm = nc.tensor.matmul(gb[:, 2 * k + cls, :], fwd[:, 2 + cls, k, j, :], source[j],
                                                      start=(j == 0), stop=(j == 1))
                    mm.then_inc(v_neg_mm, 1)
                if back:
                    pe.wait_ge(w_folded, n)
                    transform(ga, 0, [w_even[:, 0, :], w_even[:, 1, :]], 0)
                    transform(ga, 1, [w_odd[:, 0, :], w_odd[:, 1, :]], 1).then_inc(w_cyc_mm, 1)
                    pe.wait_ge(w_quads, n)
                    if front:
                        pe.wait_ge(vn_moved, n + 1)
                    else:
                        pe.wait_ge(near_added, n - 1)
                        pe.wait_ge(far_moved, n - 1)
                    for cls in range(2):
                        mm = transform(gb, 2 + cls, [w_quad[:, 2 * cls, :], w_quad[:, 2 * cls + 1, :]], cls)
                    mm.then_inc(w_neg_mm, 1)
                if front:
                    pe.wait_ge(prod_added, n + 1)
                    if back:
                        pe.wait_ge(zc_terms, n)
                    else:
                        pe.wait_ge(vc_moved, n + 1)
                    for g in range(SUB):
                        for cls in range(2):
                            for k in range(2):
                                mm = nc.tensor.matmul(ga[:, g, cls * 2 * T:(cls + 1) * 2 * T],
                                                        prod[:, 2 * k + cls, g * T:(g + 1) * T],
                                                        inv[:, cls, k, :], start=(k == 0), stop=(k == 1))
                    mm.then_inc(corr_mm, 1)
                if back:
                    pe.wait_ge(zc_added, n)
                    pe.wait_ge(zn_terms, n)
                    for half in range(2):
                        for j in range(2):
                            for k in range(2):
                                nc.tensor.matmul(gb[:, 2 * half + j, :], outm[:, half, j, 0, k, :],
                                                 zc[:, 2 * k + half, :], start=(k == 0), stop=False)
                    pe.wait_ge(zn_added, n)
                    for half in range(2):
                        for j in range(2):
                            for cls in range(2):
                                for k in range(2):
                                    mm = nc.tensor.matmul(gb[:, 2 * half + j, :], outm[:, half, j, 1 + cls, k, :],
                                                            zn[:, 2 * k + cls, :], start=False,
                                                            stop=(cls == 1 and k == 1))
                    mm.then_inc(out_mm, 1)

            run(pe, before, step)

        @block.scalar
        def _(act):
            def normalise(b, c):
                n = 4 * b + c
                if isinstance(n, int) and n >= N:
                    return
                act.wait_ge(x_in[c % 4], 16 * (b + c // 4 + 1))
                at_least(act, q_mm, n)
                if c % 4 == 0:
                    at_least(act, stat_done, b + c // 4)
                for k in range(TB):
                    op = nc.scalar.activation(qs[:, k, :], xs[c % 4][:, k, :], ACT.Identity,
                                              bias=stat[:, 1, k:k + 1], scale=stat[:, 0, k:k + 1])
                op.then_inc(q_normed, 1)

            def before():
                act.wait_ge(mask_set, 2)
                normalise(0, 0)

            def step(b, c, front, back):
                n = 4 * b + c
                if front:
                    act.wait_ge(v_cyc_mm, n + 1)
                    at_least(act, zc_terms, n - 1)
                    dst = vc[c % 2]
                    nc.scalar.activation(dst[:, 4, :], ga[:, 0, :], ACT.Copy).then_inc(twin_copied, 1)
                    nc.scalar.activation(dst[:, 0:2, :], ga[:, 0:2, :], ACT.Copy)
                    nc.scalar.activation(dst[:, 2, :], ga[:, 2, :], ACT.Copy, scale=rows_but_0[:, 0:1])
                    nc.scalar.activation(dst[:, 3, :], ga[:, 3, :], ACT.Copy)
                    act.wait_ge(twin_copied, n + 1)
                    nc.scalar.activation(dst[0:1, 4, :], ga[0:1, 2, :], ACT.Copy).then_inc(vc_moved, 1)
                if back:
                    act.wait_ge(turned, n)
                    at_least(act, w_quads, n - 1)
                    nc.scalar.activation(w_high[:, :, :], ga[:, 2:4, :], ACT.Copy).then_inc(high_moved, 1)
                if front:
                    if c % 4 == 3 and not (isinstance(n, int) and n + TB >= TILES):
                        act.wait_ge(var_done, b + c // 4 + 1)
                        nc.scalar.activation(root[:, :], veps[:, :], ACT.Sqrt).then_inc(root_done, 1)
                    normalise(b, c + 1)
                    act.wait_ge(v_neg_mm, n + 1)
                    at_least(act, zn_terms, n - 1)
                    nc.scalar.activation(vn[c % 2][:, :, :], gb[:, :, :], ACT.Copy).then_inc(vn_moved, 1)
                    act.wait_ge(corr_mm, n + 1)
                    at_least(act, x1_ready, n - 1)
                    nc.scalar.activation(side[:, :, :].rearrange("p a (s l) -> p (a s) l", l=2 * T),
                                         ga[:, :, 2 * T:4 * T], ACT.Copy).then_inc(odd_moved, 1)
                    act.wait_ge(max_negated, n + 1)
                    at_least(act, turned, n)
                    for g in range(SUB):
                        nc.scalar.activation(wts[:, g, :], corr[:, g, :], ACT.Exp, bias=minus_max[:, g:g + 1]
                                             ).then_inc(exp_done, 1)
                    act.wait_ge(share_known, n + 1)
                    for g in range(SUB):
                        mm = nc.scalar.activation(wts[:, g, :], wts[:, g, :], ACT.Copy, scale=share[:, g:g + 1])
                    mm.then_inc(weights_done, 1)
                if back:
                    act.wait_ge(out_mm, n)
                    if front:
                        act.wait_ge(corr_folded, n + 1)
                    else:
                        act.wait_ge(x1_ready, n - 1)
                    nc.scalar.activation(side[:, :, :], gb[:, 2:4, :], ACT.Copy).then_inc(far_moved, 1)

            run(act, before, step)

        @block.gpsimd
        def _(pool):
            def fold(b, c):
                n = 4 * b + c
                if isinstance(n, int) and n >= N:
                    return
                v = vs[c % 2]
                pool.wait_ge(v_in[c % 2], 64 * b + 32 * (c // 2 + 1))
                at_least(pool, v_neg_mm, n)
                nc.gpsimd.tensor_tensor(v_even[:, :, :], v[:, 0:2, :], v[:, 2:4, :], ALU.add).then_inc(v_summed, 1)
                pool.wait_ge(v_summed, n + 1)
                nc.gpsimd.tensor_tensor(v[:, 0:2, :], v[:, 0:2, :], v[:, 2:4, :], ALU.subtract).then_inc(v_folded, 1)
                pool.wait_ge(q_normed, n + 1)
                nc.gpsimd.tensor_tensor(q_even[:, :, :], qs[:, 0:2, :], qs[:, 2:4, :], ALU.add).then_inc(q_summed, 1)
                pool.wait_ge(q_summed, n + 1)
                nc.gpsimd.tensor_tensor(qs[:, 0:2, :], qs[:, 0:2, :], qs[:, 2:4, :], ALU.subtract
                                        ).then_inc(q_folded, 1)
                pool.wait_ge(v_folded, n + 1)
                for k in range(2, 4):
                    op = nc.gpsimd.tensor_tensor(v[:, k, :], v[:, k, :], last[c % 2][:, :], ALU.subtract)
                op.then_inc(v_lowered, 1)

            def add_terms(terms_ready, added, count, spectrum):
                pool.wait_ge(terms_ready, count)
                nc.gpsimd.tensor_tensor(spectrum[:, 0:2, :], spectrum[:, 0:2, :], term[:, 0:2, :], ALU.add)
                nc.gpsimd.tensor_tensor(spectrum[:, 2:4, :], spectrum[:, 2:4, :], term[:, 2:4, :], ALU.subtract
                                        ).then_inc(added, 1)

            def before():
                nc.gpsimd.memset(rows_but_0[:, :], 1.0).then_inc(mask_set, 1)
                pool.wait_ge(mask_set, 1)
                nc.gpsimd.memset(rows_but_0[0:1, :], 0.0).then_inc(mask_set, 1)
                fold(0, 0)

            def step(b, c, front, back):
                n = 4 * b + c
                if front:
                    add_terms(prod_terms, prod_added, n + 1, prod)
                if back:
                    add_terms(zc_terms, zc_added, n, zc)
                    add_terms(zn_terms, zn_added, n, zn)
                if front:
                    fold(b, c + 1)
                if back:
                    xk = xs[(c - 1) % 4]
                    pool.wait_ge(far_moved, n)
                    pool.wait_ge(near_added, n)
                    nc.gpsimd.tensor_tensor(xk[:, 0:2, :], xk[:, 0:2, :], side[:, :, :], ALU.add)
                    nc.gpsimd.tensor_tensor(xk[:, 2:4, :], xk[:, 2:4, :], side[:, :, :], ALU.subtract
                                            ).then_inc(x1_ready, 1)

            run(pool, before, step)

        @block.vector
        def _(dve):
            def multiply(r, i, vr, vi, spectrum, twin, half=None):
                mul = lambda o, a, s: nc.vector.tensor_tensor(o, a, s, ALU.mult)
                mul(spectrum[:, 0:2, :], r, vr)
                op = mul(term[:, 2:4, :], r, vi)
                if half is not None:
                    op.then_inc(half, 1)
                if twin is None:
                    mul(spectrum[:, 2:4, :], i, vr)
                else:
                    mul(spectrum[:, 2, :], i[:, 0, :], twin)
                    mul(spectrum[:, 3, :], i[:, 1, :], vr[:, 1, :])
                return mul(term[:, 0:2, :], i, vi)

            def quads(b, c):
                n = 4 * b + c
                v = vs[c % 2]
                stt = lambda o, a, scalar, s, op1: nc.vector.scalar_tensor_tensor(
                    out=o, in0=a, scalar=scalar, in1=s, op0=ALU.mult, op1=op1)
                dve.wait_ge(v_lowered, n + 1)
                dve.wait_ge(v_cyc_mm, n + 1)
                stt(v_even[:, 1, :], last[c % 2][:, :], -2.0, v_even[:, 1, :], ALU.add).then_inc(v_shifted, 1)
                stt(v[:, 3, :], v[:, 3, :], -ROOT2, v[:, 0, :], ALU.add)
                dve.wait_ge(v_shifted, n + 1)
                stt(v[:, 2, :], v[:, 2, :], ROOT2, v_even[:, 1, :], ALU.add).then_inc(v_plus, 1)
                dve.wait_ge(v_plus, n + 1)
                stt(v[:, 0, :], v[:, 0, :], 2.0, v[:, 3, :], ALU.subtract)
                stt(v_even[:, 1, :], v_even[:, 1, :], 2.0, v[:, 2, :], ALU.subtract).then_inc(v_quads, 1)

            def statistics(b, c):
                n = 4 * b + c
                if isinstance(n, int) and n + TB >= TILES:
                    return
                dve.wait_ge(rows_in, 16 * (n + 1))
                for j in range(4):
                    op = nc.vector.bn_stats(bn[:, j, :], rows[:, j * CH:(j + 1) * CH])
                op.then_inc(rows_read, 1)
                wait_apart(nc, dve, rows_read, n + 1, idle[:, 2 * SUB + 2:2 * SUB + 3])
                nc.vector.bn_aggr(mv[:, c % 4, :], bn[:, :, :].rearrange("p a s -> p (a s)")).then_inc(rows_done, 1)
                dve.wait_ge(rows_done, n + 1)
                if c % 4 == 3:
                    m = b + c // 4
                    nc.vector.tensor_scalar(veps[:, :], mv[:, :, 1], EPS, None, ALU.add).then_inc(var_done, 1)
                    return m

            def close_statistics(m, n):
                dve.wait_ge(q_normed, n + 1)
                inverse_root(nc, dve, lambda: dve.wait_ge(root_done, m + 1), veps[:, :], root[:, :], r0[:, :],
                             sq[:, :], stat[:, 0, :], 1.0, root_link, 4 * m).then_inc(gain_done, 1)
                dve.wait_ge(gain_done, m + 1)
                nc.vector.scalar_tensor_tensor(out=stat[:, 1, :], in0=mv[:, :, 0], scalar=-1.0, in1=stat[:, 0, :],
                                               op0=ALU.mult, op1=ALU.mult).then_inc(stat_done, 1)
                dve.wait_ge(stat_done, m + 1)

            def choose(n):
                wait_apart(nc, dve, corr_folded, n + 1, idle[:, 0:1])
                for g in range(SUB):
                    mm = nc.vector.max(top_a[:, g, :], corr[:, g, :])
                mm.then_inc(top_a_found, 1)
                dve.wait_ge(top_a_found, n + 1)
                nc.vector.tensor_scalar(minus_max[:, :], top_a[:, :, 0], -1.0, None, ALU.mult).then_inc(max_negated, 1)
                for g in range(SUB):
                    wait_apart(nc, dve, exp_done, SUB * n + g + 1, idle[:, 1 + g:2 + g])
                    nc.vector.match_replace(corr[:, g, :], top_a[:, g, :], corr[:, g, :], NEG
                                            ).then_inc(first_marked, 1)
                for g in range(SUB):
                    wait_apart(nc, dve, first_marked, SUB * n + g + 1, idle[:, 1 + SUB + g:2 + SUB + g])
                    mm = nc.vector.max(top_b[:, g, :], corr[:, g, :])
                mm.then_inc(top_b_found, 1)
                dve.wait_ge(top_b_found, n + 1)
                nc.vector.memset(top_b[:, :, KEPT2:8], NEG).then_inc(top_b_cut, 1)
                wait_apart(nc, dve, top_b_cut, n + 1, idle[:, 1 + 2 * SUB:2 + 2 * SUB])
                for g in range(SUB):
                    nc.vector.match_replace(corr[:, g, :], top_b[:, g, :], corr[:, g, :], NEG
                                            ).then_inc(all_marked, 1)
                for g in range(SUB):
                    dve.wait_ge(all_marked, SUB * n + g + 1)
                    mm = nc.vector.scalar_tensor_tensor(out=wts[:, g, :], in0=corr[:, g, :], scalar=NEG,
                                                          in1=wts[:, g, :], op0=ALU.is_le, op1=ALU.mult,
                                                          accum_out=total[:, g:g + 1])
                mm.then_inc(kept, 1)
                dve.wait_ge(kept, n + 1)
                nc.vector.reciprocal(share[:, :], total[:, :]).then_inc(share_known, 1)

            def step(b, c, front, back):
                n = 4 * b + c
                if front:
                    quads(b, c)
                    vk = vc[c % 2]
                    dve.wait_ge(q_mm, n + 1)
                    dve.wait_ge(vc_moved, n + 1)
                    at_least(dve, corr_mm, n)
                    at_least(dve, zn_added, n - 1)
                    multiply(gb[:, 0:2, :], gb[:, 2:4, :], vk[:, 0:2, :], vk[:, 2:4, :], prod, vk[:, 4, :],
                             prod_half
                             ).then_inc(prod_terms, 1)
                if back:
                    dve.wait_ge(high_moved, n)
                    at_least(dve, w_cyc_mm, n - 1)
                    nc.vector.tensor_tensor(w_even[:, :, :], ga[:, 0:2, :], w_high[:, :, :], ALU.add)
                    nc.vector.tensor_tensor(w_odd[:, :, :], ga[:, 0:2, :], w_high[:, :, :], ALU.subtract
                                            ).then_inc(w_folded, 1)
                    dve.wait_ge(w_folded, n)
                    at_least(dve, w_neg_mm, n - 1)
                    for cls, sign in enumerate((1.0, -1.0)):
                        nc.vector.scalar_tensor_tensor(out=w_quad[:, 2 * cls, :], in0=w_high[:, 1, :],
                                                       scalar=-sign * ROOT2, in1=w_odd[:, 0, :],
                                                       op0=ALU.mult, op1=ALU.add)
                        mm = nc.vector.scalar_tensor_tensor(out=w_quad[:, 2 * cls + 1, :], in0=w_high[:, 0, :],
                                                              scalar=sign * ROOT2, in1=w_even[:, 1, :],
                                                              op0=ALU.mult, op1=ALU.add)
                    mm.then_inc(w_quads, 1)
                if front:
                    m = statistics(b, c)
                    if m is not None:
                        close_statistics(m, n)
                if back:
                    vk = vc[(c - 1) % 2]
                    dve.wait_ge(w_cyc_mm, n)
                    at_least(dve, out_mm, n - 1)
                    if front:
                        dve.wait_ge(prod_added, n + 1)
                    else:
                        dve.wait_ge(zn_added, n - 1)
                    multiply(ga[:, 0:2, :], ga[:, 2:4, :], vk[:, 0:2, :], vk[:, 2:4, :], zc, vk[:, 4, :]
                             ).then_inc(zc_terms, 1)
                    vk = vn[(c - 1) % 2]
                    dve.wait_ge(w_neg_mm, n)
                    dve.wait_ge(zc_added, n)
                    multiply(gb[:, 0:2, :], gb[:, 2:4, :], vk[:, 0:2, :], vk[:, 2:4, :], zn, None
                             ).then_inc(zn_terms, 1)
                if front:
                    dve.wait_ge(odd_moved, n + 1)
                    at_least(dve, kept, n)
                    odd = side[:, :, :].rearrange("p a (s l) -> p (a s) l", l=2 * T)
                    nc.vector.tensor_tensor(corr[:, :, 0:2 * T], ga[:, :, 0:2 * T], odd, ALU.add)
                    nc.vector.tensor_tensor(corr[:, :, 2 * T:L], ga[:, :, 0:2 * T], odd, ALU.subtract
                                            ).then_inc(corr_folded, 1)
                    choose(n)
                if back:
                    xk = xs[(c - 1) % 4]
                    dve.wait_ge(out_mm, n)
                    nc.vector.tensor_tensor(xk[:, 0:2, :], gb[:, 0:2, :], xk[:, 0:2, :], ALU.add)
                    nc.vector.tensor_tensor(xk[:, 2:4, :], gb[:, 0:2, :], xk[:, 2:4, :], ALU.add
                                            ).then_inc(near_added, 1)

            run(dve, lambda: None, step)


def feed(nc, x1, bias, whi, wlo, wscale, ident, out):
    x_rows = x1.rearrange("b l d -> (b l) d")
    out_rows = out.rearrange("b l d -> (b l) d")
    G = 4
    OC = D // CH
    TG = CH // T
    with ExitStack() as ctx:
        sb = lambda name, shape, dt=F32: ctx.enter_context(nc.sbuf_tensor(name, shape, dt))
        sem = lambda name: ctx.enter_context(nc.semaphore(name))
        w_hi = sb("f_whi", [T, OT, DB, T], F16)
        w_lo = sb("f_wlo", [T, OT, DB, T], F16)
        ident_sb = sb("f_ident", [T, T])
        bias_sb = sb("f_bias", [T, D])
        scale_sb = sb("f_scale", [T, D])
        xs = [sb(f"f_x{i}", [T, D]) for i in range(G)]
        h = sb("f_h", [T, D])
        h_hi = [sb(f"f_hhi{i}", [T, DB, T], F16) for i in range(2)]
        h_lo = [sb(f"f_hlo{i}", [T, DB, T], F16) for i in range(2)]
        y = [sb(f"f_y{i}", [T, CH]) for i in range(2)]
        bn = sb("f_bn", [T, 4, 6])
        idle = sb("f_idle", [1, 1])
        mv = sb("f_mv", [T, 2])
        veps = sb("f_veps", [T, 1])
        root = sb("f_root", [T, 1])
        r0 = sb("f_r0", [T, 1])
        sq = sb("f_sq", [T, 1])
        gain = sb("f_gain", [T, 1])
        shift = sb("f_shift", [T, 1])
        out_ps = ctx.enter_context(nc.psum_tensor("f_out", [T, OC, CH], F32))
        t_ps = ctx.enter_context(nc.psum_tensor("f_t", [T, DB, T], F32))

        const_in = sem("f_const_in")
        ident_in = sem("f_ident_in")
        w_in = [sem(f"f_w_in{i}") for i in range(OC)]
        x_in = [sem(f"f_x_in{i}") for i in range(G)]
        x_out = [sem(f"f_x_out{i}") for i in range(G)]
        link = sem("f_link")
        var_done = sem("f_var_done")
        root_done = sem("f_root_done")
        stats_done = sem("f_stats_done")
        h_done = sem("f_h_done")
        h_turned = sem("f_h_turned")
        hi_done = sem("f_hi_done")
        lo_done = sem("f_lo_done")
        out_mm = sem("f_out_mm")
        y_done = sem("f_y_done")
        bias_added = sem("f_bias_added")
        y_added = sem("f_y_added")
        block = ctx.enter_context(nc.Block())

        def run(engine, step):
            step(0, 0)
            step(0, 1)
            with engine.Fori(0, TILES // G - 1) as b:
                for c in range(2, G + 2):
                    step(b, c)
            for c in range(2, G):
                step(TILES // G - 1, c)

        @block.sync
        def _(sp):
            def load(b, c):
                n = G * b + c
                if isinstance(n, int) and n >= TILES:
                    return
                at_least(sp, x_out[c % G], 16 * (b + c // G))
                sp.dma_start(xs[c % G][:, :], x_rows[bass.ts(n, T), :]).then_inc(x_in[c % G], 16)

            def store(b, c):
                sp.wait_ge(y_added, OC * (G * b + c + 1))
                sp.dma_start(out_rows[bass.ts(G * b + c, T), :], xs[c % G][:, :]).then_inc(x_out[c % G], 16)

            load(0, 0)
            sp.dma_start(ident_sb[:, :], ident).then_inc(ident_in, 16)
            load(0, 1)
            for o in range(OC):
                part = slice(o * TG, (o + 1) * TG)
                sp.dma_start(w_hi[:, part], whi[:, part]).then_inc(w_in[o], 16)
                sp.dma_start(w_lo[:, part], wlo[:, part]).then_inc(w_in[o], 16)
                if o == 0:
                    sp.dma_start(bias_sb[:, :], bias.partition_broadcast(T)).then_inc(const_in, 16)
                    sp.dma_start(scale_sb[:, :], wscale.partition_broadcast(T)).then_inc(const_in, 16)
            load(0, 2)

            def step(b, c):
                load(b, c + 3)
                store(b, c)

            step(0, 0)
            with sp.Fori(0, TILES // G - 1) as b:
                for c in range(1, G + 1):
                    step(b, c)
            for c in range(1, G):
                step(TILES // G - 1, c)
            for i in range(G):
                sp.wait_ge(x_out[i], 16 * (TILES // G))

        @block.vector
        def _(dve):
            LINKS = 6

            def statistics(b, c):
                n = G * b + c
                if isinstance(n, int) and n >= TILES:
                    return
                dve.wait_ge(x_in[c % G], 16 * (b + c // G + 1))
                at_least(dve, h_done, n)
                for j in range(4):
                    last = nc.vector.bn_stats(bn[:, j, :], xs[c % G][:, j * CH:(j + 1) * CH])
                last.then_inc(link, 1)
                wait_apart(nc, dve, link, LINKS * n + 1, idle[:, :])
                nc.vector.bn_aggr(mv[:, :], bn[:, :, :].rearrange("p a s -> p (a s)")).then_inc(link, 1)
                dve.wait_ge(link, LINKS * n + 2)
                nc.vector.tensor_scalar(veps[:, :], mv[:, 1:2], EPS, None, ALU.add).then_inc(var_done, 1)
                dve.wait_ge(root_done, n + 1)
                nc.vector.reciprocal(r0[:, :], root[:, :]).then_inc(link, 1)
                dve.wait_ge(link, LINKS * n + 3)
                nc.vector.tensor_tensor(sq[:, :], r0[:, :], r0[:, :], ALU.mult).then_inc(link, 1)
                dve.wait_ge(link, LINKS * n + 4)
                nc.vector.tensor_tensor(sq[:, :], sq[:, :], veps[:, :], ALU.mult).then_inc(link, 1)
                dve.wait_ge(link, LINKS * n + 5)
                nc.vector.tensor_scalar(sq[:, :], sq[:, :], -0.5 * H_SCALE, 1.5 * H_SCALE, ALU.mult, ALU.add
                                        ).then_inc(link, 1)
                dve.wait_ge(link, LINKS * n + 6)
                nc.vector.tensor_tensor(gain[:, :], r0[:, :], sq[:, :], ALU.mult).then_inc(stats_done, 1)
                dve.wait_ge(stats_done, 2 * n + 1)
                nc.vector.scalar_tensor_tensor(out=shift[:, :], in0=mv[:, 0:1], scalar=-1.0, in1=gain[:, :],
                                               op0=ALU.mult, op1=ALU.mult).then_inc(stats_done, 1)

            def low(b, c):
                n = G * b + c
                if isinstance(n, int) and n >= TILES:
                    return
                dve.wait_ge(hi_done, n + 1)
                at_least(dve, out_mm, OC * (n - 1))
                nc.vector.tensor_tensor(h_lo[c % 2][:, :, :], t_ps[:, :, :], h_hi[c % 2][:, :, :], ALU.subtract
                                        ).then_inc(lo_done, 1)

            def rescale(b, c, o):
                n = G * b + c
                dve.wait_ge(out_mm, OC * n + o + 1)
                at_least(dve, y_added, OC * n + o - 1)
                nc.vector.tensor_tensor(y[o % 2][:, :], out_ps[:, o, :], scale_sb[:, o * CH:(o + 1) * CH], ALU.mult
                                        ).then_inc(y_done, 1)

            def step(b, c):
                rescale(b, c, 0)
                statistics(b, c + 2)
                rescale(b, c, 1)
                low(b, c + 1)
                rescale(b, c, 2)
                rescale(b, c, 3)

            statistics(0, 0)
            low(0, 0)
            statistics(0, 1)
            dve.wait_ge(const_in, 32)
            run(dve, step)

        @block.scalar
        def _(act):
            def take_root(b, c):
                n = G * b + c
                if isinstance(n, int) and n >= TILES:
                    return
                act.wait_ge(var_done, n + 1)
                nc.scalar.activation(root[:, :], veps[:, :], ACT.Sqrt).then_inc(root_done, 1)

            def normalise(b, c):
                n = G * b + c
                if isinstance(n, int) and n >= TILES:
                    return
                act.wait_ge(stats_done, 2 * n + 2)
                at_least(act, h_turned, n)
                nc.scalar.activation(h[:, :], xs[c % G][:, :], ACT.Identity, bias=shift[:, 0:1], scale=gain[:, 0:1]
                                     ).then_inc(h_done, 1)

            def high(b, c):
                n = G * b + c
                if isinstance(n, int) and n >= TILES:
                    return
                act.wait_ge(h_turned, n + 1)
                at_least(act, out_mm, OC * (n - 1))
                nc.scalar.activation(h_hi[c % 2][:, :, :], t_ps[:, :, :], ACT.Copy).then_inc(hi_done, 1)

            def step(b, c):
                take_root(b, c + 2)
                high(b, c + 1)
                normalise(b, c + 2)

            take_root(0, 0)
            normalise(0, 0)
            high(0, 0)
            take_root(0, 1)
            normalise(0, 1)
            run(act, step)

        @block.tensor
        def _(pe):
            def turn(b, c):
                n = G * b + c
                if isinstance(n, int) and n >= TILES:
                    return
                pe.wait_ge(h_done, n + 1)
                at_least(pe, lo_done, n)
                for k in range(DB):
                    last = nc.tensor.transpose(t_ps[:, k, :], h[:, k * T:(k + 1) * T], ident_sb[:, :])
                last.then_inc(h_turned, 1)

            def product(b, c, o):
                n = G * b + c
                at_least(pe, y_done, OC * (n - 1) + o + 1)
                part = slice(o * TG, (o + 1) * TG)
                for k in range(DB):
                    nc.tensor.matmul(out_ps[:, o, :], h_hi[c % 2][:, k, :], w_hi[:, part, k, :],
                                     start=(k == 0), stop=False)
                    nc.tensor.matmul(out_ps[:, o, :], h_hi[c % 2][:, k, :], w_lo[:, part, k, :],
                                     start=False, stop=False)
                    last = nc.tensor.matmul(out_ps[:, o, :], h_lo[c % 2][:, k, :], w_hi[:, part, k, :],
                                            start=False, stop=(k == DB - 1))
                last.then_inc(out_mm, 1)

            def step(b, c):
                n = G * b + c
                first = isinstance(n, int) and n == 0
                pe.wait_ge(lo_done, n + 1)
                for o in range(OC):
                    if o == 1:
                        turn(b, c + 1)
                    if first:
                        pe.wait_ge(w_in[o], 32)
                    product(b, c, o)

            pe.wait_ge(ident_in, 16)
            turn(0, 0)
            run(pe, step)

        @block.gpsimd
        def _(pool):
            def add_bias(b, c):
                n = G * b + c
                if isinstance(n, int) and n >= TILES:
                    return
                pool.wait_ge(h_done, n + 1)
                nc.gpsimd.tensor_tensor(xs[c % G][:, :], xs[c % G][:, :], bias_sb[:, :], ALU.add
                                        ).then_inc(bias_added, 1)

            def step(b, c):
                n = G * b + c
                pool.wait_ge(bias_added, n + 1)
                for o in range(OC):
                    part = slice(o * CH, (o + 1) * CH)
                    pool.wait_ge(y_done, OC * n + o + 1)
                    nc.gpsimd.tensor_tensor(xs[c % G][:, part], xs[c % G][:, part], y[o % 2][:, :], ALU.add
                                            ).then_inc(y_added, 1)
                add_bias(b, c + 2)

            pool.wait_ge(const_in, 32)
            add_bias(0, 0)
            add_bias(0, 1)
            run(pool, step)


def program(nc, x, values, W, bias, A, Bf, coeffs, scales, consts, out):
    x1 = nc.dram_tensor("x1_scratch", [BATCH, L, D], F32, kind="Internal").ap()
    whi = nc.dram_tensor("whi_scratch", [T, OT, DB, T], F16, kind="Internal").ap()
    wlo = nc.dram_tensor("wlo_scratch", [T, OT, DB, T], F16, kind="Internal").ap()
    wscale = nc.dram_tensor("wscale_scratch", [D], F32, kind="Internal").ap()
    with nc.sbuf_tensor("stat", [T, 2, TB], F32) as stat:
        prepare(nc, x, W, A, Bf, coeffs, scales, consts["ident"], stat, whi, wlo, wscale)
        attend(nc, x, values, consts, stat, x1)
        feed(nc, x1, bias, whi, wlo, wscale, consts["ident"], out)


_INS = ["x", "ctx_4096", "L0_ffn_W", "L0_ffn_bias", "L0_ffn_A", "L0_ffn_Bf", "L0_ffn_coeffs", "L0_ffn_scales"]


def kernel(**inputs):
    import concourse.bacc as _bacc
    from concourse.bass_utils import run_bass_kernel_spmd as _run

    nc = _bacc.Bacc("TRN2", target_bir_lowering=False, num_devices=1, dynamic_dma_scratch_size=4096)
    arrays, args, consts = {}, [], {}
    for name in _INS:
        a = np.ascontiguousarray(inputs[name])
        arrays[f"in_{name}_dram"] = a
        args.append(nc.dram_tensor(f"in_{name}_dram", a.shape, mybir.dt.from_np(a.dtype), kind="ExternalInput").ap())
    for name, a in transform_matrices().items():
        a = np.ascontiguousarray(a.astype(np.float32))
        arrays[f"const_{name}_dram"] = a
        consts[name] = nc.dram_tensor(f"const_{name}_dram", a.shape, F32, kind="ExternalInput").ap()
    out = nc.dram_tensor("out_0_dram", (BATCH, L, D), F32, kind="ExternalOutput").ap()
    program(nc, *args, consts, out)
    r = _run(nc, [arrays], core_ids=[0])
    return r.results[0]["out_0_dram"]
```

```python
from contextlib import ExitStack

import numpy as np

import concourse.bass as bass
from concourse import mybir

F32 = mybir.dt.float32
F16 = mybir.dt.float16
I32 = mybir.dt.int32
ALU = mybir.AluOpType
ACT = mybir.ActivationFunctionType
AX = mybir.AxisListType

T = 128
BATCH, L, D = 8, 512, 2048
TB = L // T
CH = 512
CHUNKS = D // CH
N = BATCH * CHUNKS
SUB = CH // T
TOPK = int(2 * np.log(L))
KEPT2 = TOPK - 8
NEG = -3.0e38
EPS = 1e-5
ROWS = BATCH * L
TILES = ROWS // T
OT = D // T
DB = D // T
EXPERTS, RANK = 16, 16
ER = EXPERTS * RANK // T
W_SCALE = 2.0 ** 14
H_SCALE = 2.0 ** 10
ROOT2 = float(np.sqrt(2.0))
EXP_BITS = 0x7F800000
INV_BITS = 0x7F000000


def position_order():
    p = np.arange(T)
    return np.concatenate([p, 2 * T - 1 - p, L - 1 - p, 2 * T + p])


def transform_matrices():
    m = np.arange(T)
    half = np.arange(2 * T)
    plus = half[(half % 4 == 0) | (half % 4 == 3)]
    minus = half[(half % 4 == 1) | (half % 4 == 2)]
    even = np.concatenate([np.arange(0, L // 2, 4), np.arange(2, L // 2, 4)])
    omegas = [2 * np.pi * even / L, 2 * np.pi * (2 * m + 1) / L,
              np.pi * (2 * plus + 1) / L, np.pi * (2 * minus + 1) / L]

    def waves(omega, at):
        return np.stack([np.cos(np.outer(at, omega)), np.sin(np.outer(at, omega))])

    fwd = np.stack([waves(w, half) for w in omegas[1:]])
    fwd = fwd.reshape(3, 2, 2, T, T).transpose(3, 0, 1, 2, 4)
    fwd_even = waves(omegas[0], half[:T])
    fwd_even[1, :, 0] = np.cos(np.pi * half[:T])
    fwd_even = fwd_even.transpose(1, 0, 2)

    at = position_order() + 0.5
    half_cyc = np.stack([waves(w, at[:T]) for w in omegas[:2]])
    half_cyc[0, 1, :, 0] = np.sin(np.pi * at[:T])
    half_cyc = half_cyc.transpose(2, 0, 1, 3)
    half_neg = np.stack([waves(w, at[:2 * T]) for w in omegas[2:]])
    half_neg = half_neg.reshape(2, 2, 2, T, T).transpose(3, 0, 1, 2, 4)

    inv = np.stack([2 * waves(w, half).transpose(0, 2, 1) / L for w in omegas[:2]])
    inv[0, 0, 0] /= 2
    inv[0, 1, 0] = np.cos(np.pi * half) / L
    inv = inv.transpose(2, 0, 1, 3)

    full = np.stack([waves(w, at[:2 * T]).transpose(0, 2, 1) / L for w in omegas])
    full[:, 1] *= -1
    full[0, 0, 0] /= 2
    full[0, 1, 0] = np.sin(np.pi * at[:2 * T]) / (2 * L)
    parts = []
    for k in range(2):
        blocks = np.stack([full[0, k], full[1, k], full[2, 1 - k], full[3, 1 - k]]).reshape(4, T, 2, T)
        near, far = (blocks[:, :, 0] + blocks[:, :, 1]) / 2, (blocks[:, :, 0] - blocks[:, :, 1]) / 2
        parts.append([near[[k, 2, 3]], far[[1 - k, 2, 3]]])
    out = np.array(parts).transpose(3, 1, 0, 2, 4)

    return {"fwd": fwd, "fwd_even": fwd_even, "half_cyc": half_cyc, "half_neg": half_neg, "inv": inv, "out": out,
            "ident": np.eye(T)}


def at_least(engine, sem, value):
    if isinstance(value, int) and value <= 0:
        return
    engine.wait_ge(sem, value)


def wait_apart(nc, engine, sem, value, cell):
    at_least(engine, sem, value)
    nc.vector.memset(cell, 0.0)


def inverse_root(nc, dve, act_root, veps, root, r0, sq, out, gain, link, base):
    act_root()
    nc.vector.reciprocal(r0, root).then_inc(link, 1)
    dve.wait_ge(link, base + 1)
    nc.vector.tensor_tensor(sq, r0, r0, ALU.mult).then_inc(link, 1)
    dve.wait_ge(link, base + 2)
    nc.vector.tensor_tensor(sq, sq, veps, ALU.mult).then_inc(link, 1)
    dve.wait_ge(link, base + 3)
    nc.vector.tensor_scalar(sq, sq, -0.5 * gain, 1.5 * gain, ALU.mult, ALU.add).then_inc(link, 1)
    dve.wait_ge(link, base + 4)
    return nc.vector.tensor_tensor(out, r0, sq, ALU.mult)


def prepare(nc, shared, x, W, A, Bf, coeffs, scales, whi, wlo, wscale):
    x_rows = x.rearrange("b l d -> (b l) d")
    ident_sb, stat = shared.ident, shared.stat
    JC = D // CH
    with ExitStack() as ctx:
        sb = lambda name, shape, dt=F32: ctx.enter_context(nc.sbuf_tensor(name, shape, dt))
        sem = lambda name: ctx.enter_context(nc.semaphore(name))
        a_sb = sb("p_a", [T, ER, D])
        mix = sb("p_mix", [T, ER])
        mix2 = sb("p_mix2", [T, ER])
        w_sb = [sb(f"p_w{i}", [T, D]) for i in range(4)]
        b_sb = [sb(f"p_b{i}", [T, EXPERTS, RANK]) for i in range(4)]
        bt_sb = [sb(f"p_bt{i}", [T, ER, T]) for i in range(2)]
        hi_sb = [sb(f"p_hi{i}", [T, DB, T], F16) for i in range(2)]
        lo_sb = [sb(f"p_lo{i}", [T, DB, T], F16) for i in range(2)]
        x_sb = [sb(f"p_x{i}", [T, D]) for i in range(TB)]
        bn = [sb(f"p_bn{i}", [T, 4, 6]) for i in range(TB)]
        mv = sb("p_mv", [T, TB, 2])
        largest = sb("p_largest", [T, 1])
        floor2 = sb("p_floor2", [T, 1])
        inverse2 = sb("p_inverse2", [T, 1])
        up = [sb(f"p_up{i}", [T, 1]) for i in range(2)]
        down = [sb(f"p_down{i}", [T, 1]) for i in range(2)]
        root = sb("p_root", [T, TB])
        veps = sb("p_veps", [T, TB])
        r0 = sb("p_r0", [T, TB])
        sq = sb("p_sq", [T, TB])
        b_ps = ctx.enter_context(nc.psum_tensor("p_b_ps", [T, TB, T], F32))
        delta_ps = ctx.enter_context(nc.psum_tensor("p_delta", [T, 3, CH], F32))
        t_ps = ctx.enter_context(nc.psum_tensor("p_t", [T, DB, T], F32))

        const_in = sem("p_const_in")
        a_in = sem("p_a_in")
        w_in = [sem(f"p_w_in{i}") for i in range(4)]
        b_in = [sem(f"p_b_in{i}") for i in range(4)]
        x_in = [sem(f"p_x_in{i}") for i in range(TB)]
        stored = [sem(f"p_stored{i}") for i in range(2)]
        mixed = sem("p_mixed")
        b_turned = sem("p_b_turned")
        b_weighted = sem("p_b_weighted")
        delta_mm = sem("p_delta_mm")
        w_added = sem("p_w_added")
        w_scale_known = sem("p_w_scale_known")
        w_scaled = sem("p_w_scaled")
        w_turned = sem("p_w_turned")
        hi_done = sem("p_hi_done")
        lo_done = sem("p_lo_done")
        link = sem("p_link")
        rows_read = sem("p_rows_read")
        rows_done = sem("p_rows_done")
        var_done = sem("p_var_done")
        root_done = sem("p_root_done")
        delta_bank = (0, 1, 2, 1)
        freed = (1 - JC, 0, 3 - JC, 2)
        block = ctx.enter_context(nc.Block())

        def run(engine, step):
            step(0, 0)
            step(0, 1)
            with engine.Fori(0, OT // 4 - 1) as b:
                for c in range(2, 6):
                    step(b, c)
            for c in range(2, 4):
                step(OT // 4 - 1, c)

        @block.sync
        def _(sp):
            def load(b, c):
                n = 4 * b + c
                p, q = c % 2, c % 4
                at_least(sp, w_turned, n - 3)
                sp.dma_start(b_sb[q][:, :, :], Bf[:, bass.ts(n, T), :].rearrange("e o r -> o e r")
                             ).then_inc(b_in[q], 16)
                sp.dma_start(w_sb[q][:, :], W[bass.ts(n, T), :]).then_inc(w_in[q], 16)

            def store(b, c):
                n = 4 * b + c
                p, q = c % 2, c % 4
                sp.wait_ge(lo_done, n + 1)
                sp.wait_ge(hi_done, n + 1)
                sp.wait_ge(w_scale_known, n + 1)
                sp.dma_start(whi[:, bass.ds(n, 1)].rearrange("p a k o -> p (a k o)"),
                             hi_sb[p][:, :, :].rearrange("p k o -> p (k o)")).then_inc(stored[p], 16)
                sp.dma_start(wlo[:, bass.ds(n, 1)].rearrange("p a k o -> p (a k o)"),
                             lo_sb[p][:, :, :].rearrange("p k o -> p (k o)")).then_inc(stored[p], 16)
                sp.dma_start(wscale[bass.ts(n, T)].unsqueeze(1), down[p][:, :]).then_inc(stored[p], 16)

            def load_rows(k):
                sp.dma_start(x_sb[k][:, :], x_rows[k * T:(k + 1) * T, :]).then_inc(x_in[k], 16)

            sp.dma_start(ident_sb[:, :], shared.consts["ident"]).then_inc(shared.ident_in, 16)
            per = EXPERTS // ER
            for h in range(ER):
                for vec, dst in ((coeffs, mix), (scales, mix2)):
                    part = vec[h * per:(h + 1) * per].unsqueeze(1).broadcast_to([per, RANK])
                    sp.dma_start(dst[:, h:h + 1], part.unsqueeze(2)).then_inc(const_in, 16)
            load(0, 0)
            sp.dma_start(a_sb[:, :, :], A.rearrange("(h e) r d -> (e r) h d", h=ER)).then_inc(a_in, 16)
            load(0, 1)
            load_rows(0)
            load(0, 2)
            load_rows(1)

            def step(b, c):
                if not (isinstance(b, int) and 4 * b + c + 3 >= OT):
                    load(b, c + 3)
                store(b, c)

            step(0, 0)
            load_rows(2)
            load_rows(3)
            shared.load_chunk(sp, 0, 0)
            with sp.Fori(0, OT // 4 - 1) as b:
                for c in range(1, 5):
                    step(b, c)
            shared.load_chunk(sp, 0, 1)
            step(OT // 4 - 1, 1)
            shared.load_matrices(sp, 0)
            step(OT // 4 - 1, 2)
            shared.load_matrices(sp, 1)
            step(OT // 4 - 1, 3)
            for p in range(2):
                sp.wait_ge(stored[p], 48 * (OT // 2))

        @block.tensor
        def _(pe):
            def turn_b(b, c):
                n = 4 * b + c
                pe.wait_ge(b_in[c % 4], 16 * (b + c // 4 + 1))
                at_least(pe, b_weighted, n)
                flat = b_sb[c % 4][:, :, :].rearrange("o e r -> o (e r)")
                for h in range(ER):
                    last = nc.tensor.transpose(b_ps[:, h, :], flat[:, h * T:(h + 1) * T], ident_sb[:, :])
                last.then_inc(b_turned, 1)

            def weights(b, c):
                n = 4 * b + c
                p = c % 2
                pe.wait_ge(b_weighted, n + 1)
                for j in range(JC):
                    at_least(pe, w_added, JC * n + freed[j])
                    for h in range(ER):
                        last = nc.tensor.matmul(delta_ps[:, delta_bank[j], :], bt_sb[p][:, h, :],
                                                a_sb[:, h, j * CH:(j + 1) * CH],
                                                start=(h == 0), stop=(h == ER - 1))
                    last.then_inc(delta_mm, 1)

            def turn(b, c):
                n = 4 * b + c
                p, q = c % 2, c % 4
                pe.wait_ge(w_scaled, n + 1)
                at_least(pe, lo_done, n)
                for k in range(DB):
                    last = nc.tensor.transpose(t_ps[:, k, :], w_sb[q][:, k * T:(k + 1) * T], ident_sb[:, :])
                last.then_inc(w_turned, 1)

            pe.wait_ge(shared.ident_in, 16)
            turn_b(0, 0)
            turn_b(0, 1)
            pe.wait_ge(a_in, 16)
            weights(0, 0)

            def step(b, c):
                if not (isinstance(b, int) and 4 * b + c + 1 >= OT):
                    weights(b, c + 1)
                if not (isinstance(b, int) and 4 * b + c + 2 >= OT):
                    turn_b(b, c + 2)
                turn(b, c)

            run(pe, step)

        @block.scalar
        def _(act):
            def weigh(b, c):
                n = 4 * b + c
                p, q = c % 2, c % 4
                act.wait_ge(b_turned, n + 1)
                at_least(act, delta_mm, JC * (n - 1))
                for h in range(ER):
                    last = nc.scalar.activation(bt_sb[p][:, h, :], b_ps[:, h, :], ACT.Copy, scale=mix[:, h:h + 1])
                last.then_inc(b_weighted, 1)

            def scale(b, c):
                n = 4 * b + c
                p, q = c % 2, c % 4
                act.wait_ge(w_scale_known, n + 1)
                nc.scalar.activation(w_sb[q][:, :], w_sb[q][:, :], ACT.Copy, scale=up[p][:, 0:1]
                                     ).then_inc(w_scaled, 1)

            def high(b, c):
                n = 4 * b + c
                p, q = c % 2, c % 4
                act.wait_ge(w_turned, n + 1)
                at_least(act, stored[p], 48 * (2 * b + c // 2))
                nc.scalar.activation(hi_sb[p][:, :, :], t_ps[:, :, :], ACT.Copy).then_inc(hi_done, 1)

            act.wait_ge(mixed, 1)
            weigh(0, 0)
            weigh(0, 1)

            def step(b, c):
                scale(b, c)
                if not (isinstance(b, int) and 4 * b + c + 2 >= OT):
                    weigh(b, c + 2)
                high(b, c)

            run(act, step)
            act.wait_ge(var_done, 1)
            nc.scalar.activation(root[:, :], veps[:, :], ACT.Sqrt).then_inc(root_done, 1)

        @block.gpsimd
        def _(pool):
            shared.fold_values(nc, pool, 0, 0)

        @block.vector
        def _(dve):
            LINKS = 4

            def scale(b, c):
                n = 4 * b + c
                p, q = c % 2, c % 4
                dve.wait_ge(w_in[q], 16 * (b + c // 4 + 1))
                for j in range(JC):
                    dve.wait_ge(delta_mm, JC * n + j + 1)
                    part = w_sb[q][:, j * CH:(j + 1) * CH]
                    nc.vector.tensor_tensor(part, part, delta_ps[:, delta_bank[j], :], ALU.add).then_inc(w_added, 1)
                dve.wait_ge(w_added, JC * n + JC)
                nc.vector.tensor_reduce(largest[:, :], w_sb[q][:, :], AX.X, ALU.max,
                                        apply_absolute_value=True).then_inc(link, 1)
                dve.wait_ge(link, LINKS * n + 1)
                nc.vector.tensor_scalar(largest[:, :], largest[:, :], 2.0 ** -100, None, ALU.max).then_inc(link, 1)
                dve.wait_ge(link, LINKS * n + 2)
                nc.vector.tensor_scalar(floor2[:, :].bitcast(I32), largest[:, :].bitcast(I32), EXP_BITS, None,
                                        ALU.bitwise_and).then_inc(link, 1)
                dve.wait_ge(link, LINKS * n + 3)
                nc.vector.tensor_scalar(inverse2[:, :].bitcast(I32), floor2[:, :].bitcast(I32), -1.0,
                                        float(INV_BITS), ALU.mult, ALU.add).then_inc(link, 1)
                dve.wait_ge(link, LINKS * n + 4)
                at_least(dve, w_scaled, n - 1)
                at_least(dve, stored[p], 48 * (2 * b + c // 2))
                nc.vector.tensor_scalar(down[p][:, :], floor2[:, :], 1.0 / (W_SCALE * H_SCALE), None, ALU.mult)
                nc.vector.tensor_scalar(up[p][:, :], inverse2[:, :], W_SCALE, None, ALU.mult
                                        ).then_inc(w_scale_known, 1)

            def low(b, c):
                n = 4 * b + c
                p, q = c % 2, c % 4
                dve.wait_ge(hi_done, n + 1)
                at_least(dve, stored[p], 48 * (2 * b + c // 2))
                nc.vector.tensor_tensor(lo_sb[p][:, :, :], t_ps[:, :, :], hi_sb[p][:, :, :], ALU.subtract
                                        ).then_inc(lo_done, 1)

            dve.wait_ge(const_in, 32 * ER)
            nc.vector.tensor_tensor(mix[:, :], mix[:, :], mix2[:, :], ALU.mult).then_inc(mixed, 1)

            def statistics(k):
                dve.wait_ge(x_in[k], 16)
                for j in range(4):
                    op = nc.vector.bn_stats(bn[k][:, j, :], x_sb[k][:, j * CH:(j + 1) * CH])
                return op

            def step(b, c):
                scale(b, c)
                if not (isinstance(b, int) and 4 * b + c == 0):
                    low(b, c - 1)
                if isinstance(b, int) and b == 0:
                    statistics(c)

            run(dve, step)
            statistics(2)
            statistics(3).then_inc(rows_read, 1)
            dve.wait_ge(rows_read, 1)
            for k in range(TB):
                last = nc.vector.bn_aggr(mv[:, k, :], bn[k][:, :, :].rearrange("p a s -> p (a s)"))
            last.then_inc(rows_done, 1)
            dve.wait_ge(rows_done, 1)
            nc.vector.tensor_scalar(veps[:, :], mv[:, :, 1], EPS, None, ALU.add).then_inc(var_done, 1)
            low(OT // 4 - 1, 3)
            k = LINKS * OT
            inverse_root(nc, dve, lambda: dve.wait_ge(root_done, 1), veps[:, :], root[:, :], r0[:, :], sq[:, :],
                         stat[:, 0, :], 1.0, link, k).then_inc(link, 1)
            dve.wait_ge(link, k + 5)
            nc.vector.scalar_tensor_tensor(out=stat[:, 1, :], in0=mv[:, :, 0], scalar=-1.0, in1=stat[:, 0, :],
                                           op0=ALU.mult, op1=ALU.mult).then_inc(link, 1)
            dve.wait_ge(link, k + 6)


class Shared:

    def __init__(self, nc, ctx, x, values, consts):
        sb = lambda name, shape, dt=F32: ctx.enter_context(nc.sbuf_tensor(name, shape, dt))
        self.x, self.values, self.consts = x, values, consts
        self.stat = sb("stat", [T, 2, TB])
        self.fwd = sb("fwd", [T, 3, 2, 2, T])
        self.fwd_even = sb("fwd_even", [T, 2, T])
        self.inv = sb("inv", [T, 2, 2, 2 * T])
        self.outm = sb("outm", [T, 2, 2, 3, T])
        self.half_cyc = sb("half_cyc", [T, 2, 2, T])
        self.half_neg = sb("half_neg", [T, 2, 2, 2, T])
        self.ident = sb("ident", [T, T])
        self.xs = [sb(f"xs{i}", [T, TB, CH]) for i in range(4)]
        self.vs = [sb(f"vs{i}", [T, TB, CH]) for i in range(2)]
        self.v_mean = sb("v_mean", [T, 2, CH])
        self.v_folded = ctx.enter_context(nc.semaphore("v_folded"))
        self.last = [sb(f"last{i}", [T, CH]) for i in range(2)]
        self.ident_in = ctx.enter_context(nc.semaphore("ident_in"))
        self.const_in = ctx.enter_context(nc.semaphore("const_in"))
        self.x_in = [ctx.enter_context(nc.semaphore(f"x_in{i}")) for i in range(4)]
        self.v_in = [ctx.enter_context(nc.semaphore(f"v_in{i}")) for i in range(2)]

    def load_chunk(self, sp, b, c):
        sp.dma_start(self.xs[c % 4][:, :, :], chunk_of(self.x, b, c)).then_inc(self.x_in[c % 4], 16)
        sp.dma_start(self.vs[c % 2][:, :, :], chunk_of(self.values, b, c)).then_inc(self.v_in[c % 2], 16)
        sp.dma_start(self.last[c % 2][:, :], last_row_of(self.values, b, c).partition_broadcast(T)
                     ).then_inc(self.v_in[c % 2], 16)

    def fold_values(self, nc, pool, b, c):
        v = self.vs[c % 2]
        pool.wait_ge(self.v_in[c % 2], 64 * b + 32 * (c // 2 + 1))
        nc.gpsimd.tensor_tensor(self.v_mean[:, :, :], v[:, 0:2, :], v[:, 2:4, :], ALU.add)
        nc.gpsimd.tensor_tensor(v[:, 2:4, :], v[:, 0:2, :], v[:, 2:4, :], ALU.subtract).then_inc(self.v_folded, 1)

    def load_matrices(self, sp, part):
        matrices = (("half_cyc", self.half_cyc), ("half_neg", self.half_neg), ("fwd", self.fwd),
                    ("fwd_even", self.fwd_even), ("inv", self.inv), ("out", self.outm))
        for name, dst in matrices[3 * part:3 * part + 3]:
            sp.dma_start(dst[:], self.consts[name]).then_inc(self.const_in, 16)


def batch_row(dram, b, c):
    row = b + c // CHUNKS
    return dram[row:row + 1] if isinstance(row, int) else dram[bass.ds(row, 1)]


def chunk_of(dram, b, c):
    col = (c % CHUNKS) * CH
    return batch_row(dram, b, c)[:, :, col:col + CH].rearrange("a (k p) d -> p (a k) d", p=T)


def last_row_of(dram, b, c):
    col = (c % CHUNKS) * CH
    return batch_row(dram, b, c)[:, 2 * T, col:col + CH].rearrange("a d -> (a d)")


def attend(nc, shared, x, x1):
    x_rows = x.rearrange("b l d -> (b l) d")
    stat, fwd, fwd_even, inv, outm, ident = (shared.stat, shared.fwd, shared.fwd_even, shared.inv, shared.outm,
                                             shared.ident)
    v_mean, v_folded = shared.v_mean, shared.v_folded
    half_cyc, half_neg = shared.half_cyc, shared.half_neg
    xs, vs, last, x_in, v_in = shared.xs, shared.vs, shared.last, shared.x_in, shared.v_in
    with ExitStack() as ctx:
        sb = lambda name, shape, dt=F32: ctx.enter_context(nc.sbuf_tensor(name, shape, dt))
        sem = lambda name: ctx.enter_context(nc.semaphore(name))
        v_skews = sb("a_v_skews", [T, 2, CH])
        w_total = sb("a_w_total", [T, CH])
        idle = sb("a_idle", [1, 2 * SUB + 2])
        rows_but_0 = sb("a_rows_but_0", [T, 1])
        rows = sb("a_rows", [T, D])
        row_sums, minus_mean, squares = (sb(f"a_{name}", [T, TB]) for name in ("row_sums", "minus_mean", "squares"))
        veps, root, r0, sq = (sb(f"a_{name}", [T, TB]) for name in ("veps", "root", "r0", "sq"))
        qs = sb("a_q", [T, TB, CH])
        q_mean = sb("a_q_mean", [T, 2, CH])
        vc = [sb(f"a_vc{i}", [T, 5, CH]) for i in range(2)]
        vn = [sb(f"a_vn{i}", [T, 4, CH]) for i in range(2)]
        prod = sb("a_prod", [T, 4, CH])
        term = sb("a_term", [T, 4, CH])
        zc = sb("a_zc", [T, 4, CH])
        zn = sb("a_zn", [T, 4, CH])
        corr = sb("a_corr", [T, SUB, L])
        wts = sb("a_wts", [T, SUB, L])
        side = sb("a_side", [T, 2, CH])
        w_high = sb("a_w_high", [T, 2, CH])
        w_even = sb("a_w_even", [T, 2, CH])
        w_odd = sb("a_w_odd", [T, 2, CH])
        w_quad = sb("a_w_quad", [T, 4, CH])
        top_a = sb("a_top_a", [T, SUB, 8])
        top_b = sb("a_top_b", [T, SUB, 8])
        minus_max = sb("a_minus_max", [T, SUB])
        total = sb("a_total", [T, SUB])
        share = sb("a_share", [T, SUB])
        ga = ctx.enter_context(nc.psum_tensor("a_ga", [T, 4, CH], F32))
        gb = ctx.enter_context(nc.psum_tensor("a_gb", [T, 4, CH], F32))

        mask_set = sem("a_mask_set")
        x1_out = [sem(f"a_x1_out{i}") for i in range(4)]
        q_normed = sem("a_q_normed")
        vr_moved = sem("a_vr_moved")
        vi_moved = sem("a_vi_moved")
        vc_moved = sem("a_vc_moved")
        twin_copied = sem("a_twin_copied")
        high_moved = sem("a_high_moved")
        vn_moved = sem("a_vn_moved")
        odd_moved = sem("a_odd_moved")
        exp_done = sem("a_exp_done")
        low_scaled = sem("a_low_scaled")
        out_moved = sem("a_out_moved")
        q_folded = sem("a_q_folded")
        q_halved = sem("a_q_halved")
        q_split = sem("a_q_split")
        prod_added = sem("a_prod_added")
        zc_added = sem("a_zc_added")
        zn_added = sem("a_zn_added")
        skew_added = sem("a_skew_added")
        out_parted = sem("a_out_parted")
        v_cyc_mm = sem("a_v_cyc_mm")
        q_mm = sem("a_q_mm")
        turned = sem("a_turned")
        v_neg_mm = sem("a_v_neg_mm")
        w_cyc_mm = sem("a_w_cyc_mm")
        w_neg_mm = sem("a_w_neg_mm")
        corr_mm = sem("a_corr_mm")
        out_mm = sem("a_out_mm")
        prod_half = sem("a_prod_half")
        prod_terms = sem("a_prod_terms")
        x1_ready = sem("a_x1_ready")
        v_padded = sem("a_v_padded")
        w_split = sem("a_w_split")
        w_total_done = sem("a_w_total_done")
        v_halved = sem("a_v_halved")
        v_lowered = sem("a_v_lowered")
        rows_summed = sem("a_rows_summed")
        mean_known = sem("a_mean_known")
        rows_done = sem("a_rows_done")
        var_done = sem("a_var_done")
        root_link = sem("a_root_link")
        gain_done = sem("a_gain_done")
        stat_done = sem("a_stat_done")
        w_folded = sem("a_w_folded")
        w_quads = sem("a_w_quads")
        zc_terms = sem("a_zc_terms")
        zn_terms = sem("a_zn_terms")
        corr_folded = sem("a_corr_folded")
        top_a_found = sem("a_top_a_found")
        max_negated = sem("a_max_negated")
        first_marked = sem("a_first_marked")
        top_b_found = sem("a_top_b_found")
        top_b_cut = sem("a_top_b_cut")
        all_marked = sem("a_all_marked")
        kept = sem("a_kept")
        share_known = sem("a_share_known")
        high_scaled = sem("a_high_scaled")
        rows_in = sem("a_rows_in")
        root_done = sem("a_root_done")
        block = ctx.enter_context(nc.Block())

        def run(engine, before, step):
            before()
            step(0, 0, True, False)
            step(0, 1, True, True)
            with engine.Fori(0, BATCH - 2) as b:
                for c in range(2, CHUNKS + 2):
                    step(b, c, True, True)
            for c in range(2, 2 * CHUNKS):
                step(BATCH - 2, c, True, True)
            step(BATCH - 2, 2 * CHUNKS, False, True)

        @block.sync
        def _(sp):
            def load(b, c):
                n = 4 * b + c
                if isinstance(n, int) and n >= N:
                    return
                at_least(sp, v_neg_mm, n - 1)
                at_least(sp, x1_out[c % 4], 16 * (b + c // 4))
                shared.load_chunk(sp, b, c)

            def load_rows(b, c):
                n = 4 * b + c
                if isinstance(n, int) and n + TB >= TILES:
                    return
                at_least(sp, rows_done, n)
                sp.dma_start(rows[:, :], x_rows[bass.ts(n + TB, T), :]).then_inc(rows_in, 16)

            def step(b, c, front, back):
                if front:
                    load_rows(b, c)
                store(b, c - 2)
                if front:
                    load(b, c + 2)

            def store(b, c):
                n = 4 * b + c
                if isinstance(n, int) and n < 0:
                    return
                sp.wait_ge(x1_ready, n + 1)
                sp.dma_start(chunk_of(x1, b, c), xs[c % 4][:, :, :]).then_inc(x1_out[c % 4], 16)

            run(sp, lambda: None, step)
            store(BATCH - 1, 3)
            for i in range(4):
                sp.wait_ge(x1_out[i], 16 * BATCH)

        @block.tensor
        def _(pe):
            def transform_half(group, means, skews, each=None):
                for k, source in enumerate((means, skews)):
                    for cls in range(2):
                        mm = nc.tensor.matmul(group[:, 2 * k + cls, :], half_cyc[:, cls, k, :], source[:, cls, :],
                                              start=True, stop=True)
                    if each is not None:
                        mm.then_inc(each, 1)
                return mm

            def transform_even(group, total, difference):
                for k in range(2):
                    for i, source in enumerate((total, difference)):
                        part = slice(i * T // 2, (i + 1) * T // 2)
                        mm = nc.tensor.matmul(group[part, 2 * k, :], fwd_even[:, k, part], source,
                                              start=True, stop=True)
                return mm

            def transform(group, cls, source, first_bank):
                for k in range(2):
                    for j in range(2):
                        mm = nc.tensor.matmul(group[:, first_bank + 2 * k, :], fwd[:, cls, k, j, :], source[j],
                                                start=(j == 0), stop=(j == 1))
                return mm

            def before():
                pe.wait_ge(shared.const_in, 16 * 6)

            def step(b, c, front, back):
                n = 4 * b + c
                if front:
                    v = vs[c % 2]
                    pe.wait_ge(v_halved, n + 1)
                    at_least(pe, corr_folded, n)
                    transform_half(ga, v, v_skews).then_inc(v_cyc_mm, 1)
                    pe.wait_ge(q_folded, n + 1)
                    at_least(pe, out_moved, n - 1)
                    transform_half(gb, qs, q_mean, each=q_mm)
                if back:
                    pe.wait_ge(low_scaled, n)
                    pe.wait_ge(high_scaled, n)
                    if front:
                        pe.wait_ge(vc_moved, n + 1)
                    else:
                        pe.wait_ge(corr_folded, n)
                    for k in range(TB):
                        for g in range(SUB):
                            mm = nc.tensor.transpose(ga[:, k, g * T:(g + 1) * T], wts[:, g, k * T:(k + 1) * T],
                                                       ident[:, :])
                    mm.then_inc(turned, 1)
                if front:
                    pe.wait_ge(prod_half, n + 1)
                    for k, source in enumerate((v[:, 2:4, :], v_mean)):
                        if k == 1:
                            pe.wait_ge(v_lowered, n + 1)
                            pe.wait_ge(prod_terms, n + 1)
                        for cls in range(2):
                            for j in range(2):
                                mm = nc.tensor.matmul(gb[:, 2 * k + cls, :], half_neg[:, cls, k, j, :],
                                                      source[:, j, :], start=(j == 0), stop=(j == 1))
                    mm.then_inc(v_neg_mm, 1)
                if back:
                    pe.wait_ge(w_total_done, n)
                    transform_even(ga, w_total[:, :], w_even[:, 0, :])
                    transform(ga, 0, [w_odd[:, 0, :], w_odd[:, 1, :]], 1).then_inc(w_cyc_mm, 1)
                    pe.wait_ge(w_quads, n)
                    if front:
                        pe.wait_ge(vn_moved, n + 1)
                    else:
                        pe.wait_ge(out_moved, n - 1)
                    for cls in range(2):
                        mm = transform(gb, 1 + cls, [w_quad[:, 2 * cls, :], w_quad[:, 2 * cls + 1, :]], cls)
                    mm.then_inc(w_neg_mm, 1)
                if front:
                    pe.wait_ge(prod_added, n + 1)
                    if back:
                        pe.wait_ge(zc_terms, 2 * n)
                    else:
                        pe.wait_ge(vc_moved, n + 1)
                    for g in range(SUB):
                        for cls in range(2):
                            for k in range(2):
                                mm = nc.tensor.matmul(ga[:, g, cls * 2 * T:(cls + 1) * 2 * T],
                                                        prod[:, 2 * k + cls, g * T:(g + 1) * T],
                                                        inv[:, cls, k, :], start=(k == 0), stop=(k == 1))
                        if g % 2 == 1:
                            mm.then_inc(corr_mm, 1)
                if back:
                    pe.wait_ge(zc_added, n)
                    pe.wait_ge(zn_terms, 2 * n)
                    for far in range(2):
                        for k in range(2):
                            cls = far if k == 0 else 1 - far
                            nc.tensor.matmul(gb[:, 2 * far + k, :], outm[:, far, k, 0, :], zc[:, 2 * k + cls, :],
                                             start=True, stop=False)
                    pe.wait_ge(zn_added, n)
                    for far in range(2):
                        for k in range(2):
                            for cls in range(2):
                                mm = nc.tensor.matmul(gb[:, 2 * far + k, :], outm[:, far, k, 1 + cls, :],
                                                      zn[:, 2 * (1 - k) + cls, :], start=False, stop=(cls == 1))
                    mm.then_inc(out_mm, 1)

            run(pe, before, step)

        @block.scalar
        def _(act):
            def normalise(b, c):
                n = 4 * b + c
                if isinstance(n, int) and n >= N:
                    return
                act.wait_ge(x_in[c % 4], 16 * (b + c // 4 + 1))
                at_least(act, q_mm, 2 * n)
                if c % 4 == 0:
                    at_least(act, stat_done, b + c // 4)
                for k in range(TB):
                    op = nc.scalar.activation(qs[:, k, :], xs[c % 4][:, k, :], ACT.Identity,
                                              bias=stat[:, 1, k:k + 1], scale=stat[:, 0, k:k + 1])
                op.then_inc(q_normed, 1)

            def statistics(b, c):
                n = 4 * b + c
                if isinstance(n, int) and n + TB >= TILES:
                    return
                k = c % 4
                act.wait_ge(rows_in, 16 * (n + 1))
                nc.scalar.activation(rows[:, :], rows[:, :], ACT.Copy, accum_out=row_sums[:, k:k + 1]
                                     ).then_inc(rows_summed, 1)
                act.wait_ge(rows_summed, n + 1)
                nc.scalar.activation(minus_mean[:, k:k + 1], row_sums[:, k:k + 1], ACT.Copy, scale=-1.0 / D
                                     ).then_inc(mean_known, 1)
                act.wait_ge(mean_known, n + 1)
                nc.scalar.activation(rows[:, :], rows[:, :], ACT.Square, bias=minus_mean[:, k:k + 1],
                                     accum_out=squares[:, k:k + 1]).then_inc(rows_done, 1)

            def before():
                act.wait_ge(mask_set, 2)
                normalise(0, 0)

            def step(b, c, front, back):
                n = 4 * b + c
                if front:
                    act.wait_ge(v_cyc_mm, n + 1)
                    at_least(act, zc_terms, 2 * (n - 1))
                    dst = vc[c % 2]
                    nc.scalar.activation(dst[:, 0:2, :], ga[:, 0:2, :], ACT.Copy).then_inc(vr_moved, 1)
                    nc.scalar.activation(dst[:, 2, :], ga[:, 2, :], ACT.Copy, scale=rows_but_0[:, 0:1])
                    nc.scalar.activation(dst[:, 3, :], ga[:, 3, :], ACT.Copy).then_inc(vi_moved, 1)
                    nc.scalar.activation(dst[:, 4, :], ga[:, 0, :], ACT.Copy).then_inc(twin_copied, 1)
                    act.wait_ge(twin_copied, n + 1)
                    nc.scalar.activation(dst[0:1, 4, :], ga[0:1, 2, :], ACT.Copy).then_inc(vc_moved, 1)
                if back:
                    act.wait_ge(share_known, n)
                    nc.scalar.activation(wts[:, 0, :], wts[:, 0, :], ACT.Copy, scale=share[:, 0:1]
                                         ).then_inc(low_scaled, 1)
                    act.wait_ge(turned, n)
                    at_least(act, w_quads, n - 1)
                    nc.scalar.activation(w_high[:, :, :], ga[:, 2:4, :], ACT.Copy).then_inc(high_moved, 1)
                if front:
                    if c % 4 == 3 and not (isinstance(n, int) and n + TB >= TILES):
                        statistics(b, c)
                        act.wait_ge(var_done, b + c // 4 + 1)
                        nc.scalar.activation(root[:, :], veps[:, :], ACT.Sqrt).then_inc(root_done, 1)
                    normalise(b, c + 1)
                    act.wait_ge(v_neg_mm, n + 1)
                    at_least(act, zn_terms, 2 * (n - 1))
                    nc.scalar.activation(vn[c % 2][:, :, :], gb[:, :, :], ACT.Copy).then_inc(vn_moved, 1)
                    if c % 4 != 3:
                        statistics(b, c)
                    at_least(act, corr_folded, n)
                    for half in range(2):
                        act.wait_ge(corr_mm, 2 * n + half + 1)
                        nc.scalar.activation(side[:, half, :].rearrange("p (g l) -> p g l", l=2 * T),
                                             ga[:, 2 * half:2 * half + 2, 2 * T:4 * T], ACT.Copy
                                             ).then_inc(odd_moved, 1)
                    act.wait_ge(max_negated, n + 1)
                    at_least(act, turned, n)
                    for g in range(SUB):
                        nc.scalar.activation(wts[:, g, :], corr[:, g, :], ACT.Exp, bias=minus_max[:, g:g + 1]
                                             ).then_inc(exp_done, 1)
                if back:
                    act.wait_ge(out_mm, n)
                    nc.scalar.activation(zc[:, :, :], gb[:, :, :], ACT.Copy).then_inc(out_moved, 1)

            run(act, before, step)

        @block.gpsimd
        def _(pool):
            def fold_values(b, c):
                n = 4 * b + c
                if isinstance(n, int) and n >= N:
                    return
                at_least(pool, v_neg_mm, n)
                shared.fold_values(nc, pool, b, c)

            def fold_queries(b, c):
                n = 4 * b + c
                if isinstance(n, int) and n >= N:
                    return
                pool.wait_ge(q_normed, n + 1)
                nc.gpsimd.tensor_tensor(q_mean[:, :, :], qs[:, 0:2, :], qs[:, 2:4, :], ALU.add)
                nc.gpsimd.tensor_tensor(qs[:, 2:4, :], qs[:, 0:2, :], qs[:, 2:4, :], ALU.subtract
                                        ).then_inc(q_halved, 1)
                pool.wait_ge(q_halved, n + 1)
                nc.gpsimd.tensor_tensor(qs[:, 0, :], q_mean[:, 0, :], q_mean[:, 1, :], ALU.add)
                nc.gpsimd.tensor_tensor(qs[:, 1, :], q_mean[:, 0, :], q_mean[:, 1, :], ALU.subtract
                                        ).then_inc(q_split, 1)
                pool.wait_ge(q_split, n + 1)
                nc.gpsimd.tensor_tensor(q_mean[:, 0, :], qs[:, 2, :], qs[:, 3, :], ALU.subtract)
                nc.gpsimd.tensor_tensor(q_mean[:, 1, :], qs[:, 2, :], qs[:, 3, :], ALU.add).then_inc(q_folded, 1)

            def add_pairs(terms_ready, added, done, spectrum):
                for half, op in enumerate((ALU.add, ALU.subtract)):
                    part = slice(2 * half, 2 * half + 2)
                    pool.wait_ge(terms_ready, 2 * done + half - 1)
                    mm = nc.gpsimd.tensor_tensor(spectrum[:, part, :], spectrum[:, part, :], term[:, part, :], op)
                mm.then_inc(added, 1)

            def add_terms(terms_ready, added, count, spectrum):
                pool.wait_ge(terms_ready, count)
                nc.gpsimd.tensor_tensor(spectrum[:, 0:2, :], spectrum[:, 0:2, :], term[:, 0:2, :], ALU.add)
                nc.gpsimd.tensor_tensor(spectrum[:, 2:4, :], spectrum[:, 2:4, :], term[:, 2:4, :], ALU.subtract
                                        ).then_inc(added, 1)

            def before():
                nc.gpsimd.memset(rows_but_0[:, :], 1.0).then_inc(mask_set, 1)
                pool.wait_ge(mask_set, 1)
                nc.gpsimd.memset(rows_but_0[0:1, :], 0.0).then_inc(mask_set, 1)
                fold_queries(0, 0)

            def step(b, c, front, back):
                n = 4 * b + c
                if front:
                    add_terms(prod_terms, prod_added, n + 1, prod)
                    fold_values(b, c + 1)
                if back:
                    add_pairs(zc_terms, zc_added, n, zc)
                    add_pairs(zn_terms, zn_added, n, zn)
                if front:
                    fold_queries(b, c + 1)
                if back:
                    pool.wait_ge(out_moved, n)
                    by_block = zn[:, :, :].rearrange("p (k j) c -> p j k c", j=2)
                    nc.gpsimd.tensor_tensor(by_block[:, 0], zc[:, 0:2, :], zc[:, 2:4, :], ALU.add)
                    nc.gpsimd.tensor_tensor(by_block[:, 1], zc[:, 0:2, :], zc[:, 2:4, :], ALU.subtract
                                            ).then_inc(out_parted, 1)
                    xk = xs[(c - 1) % 4]
                    pool.wait_ge(out_parted, n)
                    nc.gpsimd.tensor_tensor(xk[:, 0:2, :], xk[:, 0:2, :], zn[:, 2:4, :], ALU.add)
                    nc.gpsimd.tensor_tensor(xk[:, 2:4, :], xk[:, 2:4, :], zn[:, 2:4, :], ALU.subtract
                                            ).then_inc(skew_added, 1)

            run(pool, before, step)

        @block.vector
        def _(dve):
            def multiply(r, i, vr, vi, spectrum, twin, half, terms, by_pair, front=None):
                def product(o, a, s):
                    return nc.vector.tensor_tensor(o, a, s, ALU.mult)

                product(spectrum[:, 0:2, :], r, vr)
                if front is not None:
                    dve.wait_ge(vi_moved, front + 1)
                second = (term[:, 0:2, :], i, vi), (term[:, 2:4, :], r, vi)
                if by_pair:
                    product(*second[0]).then_inc(half, 1)
                else:
                    product(*second[1]).then_inc(half, 1)
                    dve.wait_ge(q_mm, 2 * front + 2)
                    dve.wait_ge(vc_moved, front + 1)
                if twin is None:
                    product(spectrum[:, 2:4, :], i, vr)
                else:
                    product(spectrum[:, 2, :], i[:, 0, :], twin)
                    product(spectrum[:, 3, :], i[:, 1, :], vr[:, 1, :])
                product(*second[1 if by_pair else 0]).then_inc(terms, 1)

            def lower(b, c):
                n = 4 * b + c
                if isinstance(n, int) and n >= N:
                    return
                dve.wait_ge(v_folded, n + 1)
                for k in range(2):
                    op = nc.vector.scalar_tensor_tensor(out=v_mean[:, k, :], in0=last[c % 2][:, :], scalar=-2.0,
                                                        in1=v_mean[:, k, :], op0=ALU.mult, op1=ALU.add)
                op.then_inc(v_lowered, 1)

            def halve(b, c, part):
                n = 4 * b + c
                if isinstance(n, int) and n >= N:
                    return
                v, mean_0, mean_1 = vs[c % 2], v_mean[:, 0, :], v_mean[:, 1, :]
                if part == "skews":
                    at_least(dve, v_cyc_mm, n)
                    nc.vector.tensor_tensor(v_skews[:, 0, :], v[:, 2, :], v[:, 3, :], ALU.subtract)
                    nc.vector.tensor_tensor(v_skews[:, 1, :], v[:, 2, :], v[:, 3, :], ALU.add)
                if part == "sum":
                    dve.wait_ge(v_lowered, n + 1)
                    nc.vector.scalar_tensor_tensor(out=v[:, 0, :], in0=last[c % 2][:, :], scalar=float(L // T + 4),
                                                   in1=mean_0, op0=ALU.mult, op1=ALU.add).then_inc(v_padded, 1)
                    dve.wait_ge(v_padded, n + 1)
                    nc.vector.tensor_tensor(v[:, 0, :], v[:, 0, :], mean_1, ALU.add)
                if part == "difference":
                    nc.vector.tensor_tensor(v[:, 1, :], mean_0, mean_1, ALU.subtract).then_inc(v_halved, 1)

            def close_statistics(m, n):
                dve.wait_ge(rows_done, TB * (m + 1))
                nc.vector.tensor_scalar(veps[:, :], squares[:, :], 1.0 / D, EPS, ALU.mult, ALU.add
                                        ).then_inc(var_done, 1)
                dve.wait_ge(q_normed, n + 1)
                inverse_root(nc, dve, lambda: dve.wait_ge(root_done, m + 1), veps[:, :], root[:, :], r0[:, :],
                             sq[:, :], stat[:, 0, :], 1.0, root_link, 4 * m).then_inc(gain_done, 1)
                dve.wait_ge(gain_done, m + 1)
                nc.vector.tensor_tensor(stat[:, 1, :], minus_mean[:, :], stat[:, 0, :], ALU.mult
                                        ).then_inc(stat_done, 1)

            def choose(n, meanwhile):
                wait_apart(nc, dve, corr_folded, n + 1, idle[:, 0:1])
                for g in range(SUB):
                    mm = nc.vector.max(top_a[:, g, :], corr[:, g, :])
                mm.then_inc(top_a_found, 1)
                dve.wait_ge(top_a_found, n + 1)
                nc.vector.tensor_scalar(minus_max[:, :], top_a[:, :, 0], -1.0, None, ALU.mult).then_inc(max_negated, 1)
                meanwhile()
                for g in range(SUB):
                    wait_apart(nc, dve, exp_done, SUB * n + g + 1, idle[:, 1 + g:2 + g])
                    nc.vector.match_replace(corr[:, g, :], top_a[:, g, :], corr[:, g, :], NEG
                                            ).then_inc(first_marked, 1)
                for g in range(SUB):
                    wait_apart(nc, dve, first_marked, SUB * n + g + 1, idle[:, 1 + SUB + g:2 + SUB + g])
                    mm = nc.vector.max(top_b[:, g, :], corr[:, g, :])
                mm.then_inc(top_b_found, 1)
                dve.wait_ge(top_b_found, n + 1)
                nc.vector.memset(top_b[:, :, KEPT2:8], NEG).then_inc(top_b_cut, 1)
                wait_apart(nc, dve, top_b_cut, n + 1, idle[:, 1 + 2 * SUB:2 + 2 * SUB])
                for g in range(SUB):
                    nc.vector.match_replace(corr[:, g, :], top_b[:, g, :], corr[:, g, :], NEG
                                            ).then_inc(all_marked, 1)
                for g in range(SUB):
                    dve.wait_ge(all_marked, SUB * n + g + 1)
                    mm = nc.vector.scalar_tensor_tensor(out=wts[:, g, :], in0=corr[:, g, :], scalar=NEG,
                                                          in1=wts[:, g, :], op0=ALU.is_le, op1=ALU.mult,
                                                          accum_out=total[:, g:g + 1])
                mm.then_inc(kept, 1)
                dve.wait_ge(kept, n + 1)
                nc.vector.reciprocal(share[:, :], total[:, :]).then_inc(share_known, 1)
                dve.wait_ge(share_known, n + 1)
                for g in range(1, SUB):
                    mm = nc.vector.tensor_scalar(wts[:, g, :], wts[:, g, :], share[:, g:g + 1], None, ALU.mult)
                mm.then_inc(high_scaled, 1)

            def add_means(b, c):
                n = 4 * b + c
                if isinstance(n, int) and n < 0:
                    return
                xk = xs[c % 4]
                dve.wait_ge(skew_added, n + 1)
                nc.vector.tensor_tensor(xk[:, 0:2, :], zn[:, 0:2, :], xk[:, 0:2, :], ALU.add)
                nc.vector.tensor_tensor(xk[:, 2:4, :], zn[:, 0:2, :], xk[:, 2:4, :], ALU.add
                                        ).then_inc(x1_ready, 1)

            def step(b, c, front, back):
                n = 4 * b + c
                if front:
                    vk = vc[c % 2]
                    dve.wait_ge(q_mm, 2 * n + 1)
                    dve.wait_ge(vr_moved, n + 1)
                    at_least(dve, corr_mm, 2 * n)
                    at_least(dve, zn_added, n - 1)
                    multiply(gb[:, 0:2, :], gb[:, 2:4, :], vk[:, 0:2, :], vk[:, 2:4, :], prod, vk[:, 4, :],
                             prod_half, prod_terms, False, n)
                if back:
                    dve.wait_ge(high_moved, n)
                    at_least(dve, w_cyc_mm, n - 1)
                    nc.vector.tensor_tensor(w_even[:, :, :], ga[:, 0:2, :], w_high[:, :, :], ALU.add)
                    nc.vector.tensor_tensor(w_odd[:, :, :], ga[:, 0:2, :], w_high[:, :, :], ALU.subtract
                                            ).then_inc(w_folded, 1)
                    dve.wait_ge(w_folded, n)
                    nc.vector.tensor_tensor(w_total[:, :], w_even[:, 0, :], w_even[:, 1, :], ALU.add
                                            ).then_inc(w_split, 1)
                    dve.wait_ge(w_split, n)
                    nc.vector.tensor_tensor(w_even[:, 0, :], w_even[:, 0, :], w_even[:, 1, :], ALU.subtract
                                            ).then_inc(w_total_done, 1)
                    at_least(dve, w_neg_mm, n - 1)
                    for cls, sign in enumerate((1.0, -1.0)):
                        nc.vector.scalar_tensor_tensor(out=w_quad[:, 2 * cls, :], in0=w_high[:, 1, :],
                                                       scalar=-sign * ROOT2, in1=w_odd[:, 0, :],
                                                       op0=ALU.mult, op1=ALU.add)
                        mm = nc.vector.scalar_tensor_tensor(out=w_quad[:, 2 * cls + 1, :], in0=w_high[:, 0, :],
                                                              scalar=sign * ROOT2, in1=w_even[:, 1, :],
                                                              op0=ALU.mult, op1=ALU.add)
                    mm.then_inc(w_quads, 1)
                add_means(b, c - 2)
                if front and c % 4 == 3 and not (isinstance(n, int) and n + TB >= TILES):
                    close_statistics(b + c // 4, n)
                if back:
                    vk = vc[(c - 1) % 2]
                    dve.wait_ge(w_cyc_mm, n)
                    at_least(dve, x1_ready, n - 1)
                    if front:
                        dve.wait_ge(prod_added, n + 1)
                    else:
                        dve.wait_ge(zn_added, n - 1)
                    multiply(ga[:, 0:2, :], ga[:, 2:4, :], vk[:, 0:2, :], vk[:, 2:4, :], zc, vk[:, 4, :],
                             zc_terms, zc_terms, True)
                if front:
                    lower(b, c + 1)
                    halve(b, c + 1, "skews")
                if back:
                    vk = vn[(c - 1) % 2]
                    dve.wait_ge(w_neg_mm, n)
                    dve.wait_ge(zc_added, n)
                    multiply(gb[:, 0:2, :], gb[:, 2:4, :], vk[:, 0:2, :], vk[:, 2:4, :], zn, None,
                             zn_terms, zn_terms, True)
                if front:
                    halve(b, c + 1, "sum")
                    at_least(dve, high_scaled, n)
                    for half in range(2):
                        dve.wait_ge(odd_moved, 2 * n + half + 1)
                        part = slice(2 * half, 2 * half + 2)
                        odd = side[:, half, :].rearrange("p (g l) -> p g l", l=2 * T)
                        nc.vector.tensor_tensor(corr[:, part, 0:2 * T], ga[:, part, 0:2 * T], odd, ALU.add)
                        mm = nc.vector.tensor_tensor(corr[:, part, 2 * T:L], ga[:, part, 0:2 * T], odd, ALU.subtract)
                    mm.then_inc(corr_folded, 1)
                    choose(n, lambda: halve(b, c + 1, "difference"))
            def before():
                lower(0, 0)
                for part in ("skews", "sum", "difference"):
                    halve(0, 0, part)

            run(dve, before, step)
            add_means(BATCH - 1, 3)


def feed(nc, x1, bias, whi, wlo, wscale, ident, out):
    x_rows = x1.rearrange("b l d -> (b l) d")
    out_rows = out.rearrange("b l d -> (b l) d")
    G = 4
    OC = D // CH
    TG = CH // T
    with ExitStack() as ctx:
        sb = lambda name, shape, dt=F32: ctx.enter_context(nc.sbuf_tensor(name, shape, dt))
        sem = lambda name: ctx.enter_context(nc.semaphore(name))
        w_hi = sb("f_whi", [T, OT, DB, T], F16)
        w_lo = sb("f_wlo", [T, OT, DB, T], F16)
        ident_sb = sb("f_ident", [T, T])
        bias_sb = sb("f_bias", [T, D])
        scale_sb = sb("f_scale", [T, D])
        xs = [sb(f"f_x{i}", [T, D]) for i in range(G)]
        h = sb("f_h", [T, D])
        h_hi = [sb(f"f_hhi{i}", [T, DB, T], F16) for i in range(2)]
        h_lo = [sb(f"f_hlo{i}", [T, DB, T], F16) for i in range(2)]
        y = [sb(f"f_y{i}", [T, CH]) for i in range(2)]
        bn = sb("f_bn", [T, 4, 6])
        idle = sb("f_idle", [1, 1])
        mv = sb("f_mv", [T, 2])
        veps = sb("f_veps", [T, 1])
        root = sb("f_root", [T, 1])
        r0 = sb("f_r0", [T, 1])
        sq = sb("f_sq", [T, 1])
        gain = sb("f_gain", [T, 1])
        shift = sb("f_shift", [T, 1])
        out_ps = ctx.enter_context(nc.psum_tensor("f_out", [T, OC, CH], F32))
        t_ps = ctx.enter_context(nc.psum_tensor("f_t", [T, DB, T], F32))

        const_in = sem("f_const_in")
        ident_in = sem("f_ident_in")
        w_in = [sem(f"f_w_in{i}") for i in range(OC)]
        x_in = [sem(f"f_x_in{i}") for i in range(G)]
        x_out = [sem(f"f_x_out{i}") for i in range(G)]
        link = sem("f_link")
        var_done = sem("f_var_done")
        root_done = sem("f_root_done")
        stats_done = sem("f_stats_done")
        h_done = sem("f_h_done")
        h_turned = sem("f_h_turned")
        hi_done = sem("f_hi_done")
        lo_done = sem("f_lo_done")
        out_mm = sem("f_out_mm")
        y_done = sem("f_y_done")
        bias_added = sem("f_bias_added")
        y_added = sem("f_y_added")
        block = ctx.enter_context(nc.Block())

        def run(engine, step):
            step(0, 0)
            step(0, 1)
            with engine.Fori(0, TILES // G - 1) as b:
                for c in range(2, G + 2):
                    step(b, c)
            for c in range(2, G):
                step(TILES // G - 1, c)

        @block.sync
        def _(sp):
            def load(b, c):
                n = G * b + c
                if isinstance(n, int) and n >= TILES:
                    return
                at_least(sp, x_out[c % G], 16 * (b + c // G))
                sp.dma_start(xs[c % G][:, :], x_rows[bass.ts(n, T), :]).then_inc(x_in[c % G], 16)

            def store(b, c):
                sp.wait_ge(y_added, OC * (G * b + c + 1))
                sp.dma_start(out_rows[bass.ts(G * b + c, T), :], xs[c % G][:, :]).then_inc(x_out[c % G], 16)

            load(0, 0)
            sp.dma_start(ident_sb[:, :], ident).then_inc(ident_in, 16)
            for o in range(OC):
                part = slice(o * TG, (o + 1) * TG)
                sp.dma_start(w_hi[:, part], whi[:, part]).then_inc(w_in[o], 16)
                sp.dma_start(w_lo[:, part], wlo[:, part]).then_inc(w_in[o], 16)
                if o == 0:
                    load(0, 1)
                    sp.dma_start(bias_sb[:, :], bias.partition_broadcast(T)).then_inc(const_in, 16)
                    sp.dma_start(scale_sb[:, :], wscale.partition_broadcast(T)).then_inc(const_in, 16)
            load(0, 2)

            def step(b, c):
                load(b, c + 3)
                store(b, c)

            step(0, 0)
            with sp.Fori(0, TILES // G - 1) as b:
                for c in range(1, G + 1):
                    step(b, c)
            for c in range(1, G):
                step(TILES // G - 1, c)
            for i in range(G):
                sp.wait_ge(x_out[i], 16 * (TILES // G))

        @block.vector
        def _(dve):
            LINKS = 6

            def statistics(b, c):
                n = G * b + c
                if isinstance(n, int) and n >= TILES:
                    return
                dve.wait_ge(x_in[c % G], 16 * (b + c // G + 1))
                at_least(dve, h_done, n)
                for j in range(4):
                    last = nc.vector.bn_stats(bn[:, j, :], xs[c % G][:, j * CH:(j + 1) * CH])
                last.then_inc(link, 1)
                wait_apart(nc, dve, link, LINKS * n + 1, idle[:, :])
                nc.vector.bn_aggr(mv[:, :], bn[:, :, :].rearrange("p a s -> p (a s)")).then_inc(link, 1)
                dve.wait_ge(link, LINKS * n + 2)
                nc.vector.tensor_scalar(veps[:, :], mv[:, 1:2], EPS, None, ALU.add).then_inc(var_done, 1)
                dve.wait_ge(root_done, n + 1)
                nc.vector.reciprocal(r0[:, :], root[:, :]).then_inc(link, 1)
                dve.wait_ge(link, LINKS * n + 3)
                nc.vector.tensor_tensor(sq[:, :], r0[:, :], r0[:, :], ALU.mult).then_inc(link, 1)
                dve.wait_ge(link, LINKS * n + 4)
                nc.vector.tensor_tensor(sq[:, :], sq[:, :], veps[:, :], ALU.mult).then_inc(link, 1)
                dve.wait_ge(link, LINKS * n + 5)
                nc.vector.tensor_scalar(sq[:, :], sq[:, :], -0.5 * H_SCALE, 1.5 * H_SCALE, ALU.mult, ALU.add
                                        ).then_inc(link, 1)
                dve.wait_ge(link, LINKS * n + 6)
                nc.vector.tensor_tensor(gain[:, :], r0[:, :], sq[:, :], ALU.mult).then_inc(stats_done, 1)
                dve.wait_ge(stats_done, 2 * n + 1)
                nc.vector.scalar_tensor_tensor(out=shift[:, :], in0=mv[:, 0:1], scalar=-1.0, in1=gain[:, :],
                                               op0=ALU.mult, op1=ALU.mult).then_inc(stats_done, 1)

            def low(b, c):
                n = G * b + c
                if isinstance(n, int) and n >= TILES:
                    return
                dve.wait_ge(hi_done, n + 1)
                at_least(dve, out_mm, OC * (n - 1))
                nc.vector.tensor_tensor(h_lo[c % 2][:, :, :], t_ps[:, :, :], h_hi[c % 2][:, :, :], ALU.subtract
                                        ).then_inc(lo_done, 1)

            def rescale(b, c, o):
                n = G * b + c
                dve.wait_ge(out_mm, OC * n + o + 1)
                at_least(dve, y_added, OC * n + o - 1)
                nc.vector.tensor_tensor(y[o % 2][:, :], out_ps[:, o, :], scale_sb[:, o * CH:(o + 1) * CH], ALU.mult
                                        ).then_inc(y_done, 1)

            def step(b, c):
                rescale(b, c, 0)
                statistics(b, c + 2)
                rescale(b, c, 1)
                low(b, c + 1)
                rescale(b, c, 2)
                rescale(b, c, 3)

            statistics(0, 0)
            low(0, 0)
            statistics(0, 1)
            dve.wait_ge(const_in, 32)
            run(dve, step)

        @block.scalar
        def _(act):
            def take_root(b, c):
                n = G * b + c
                if isinstance(n, int) and n >= TILES:
                    return
                act.wait_ge(var_done, n + 1)
                nc.scalar.activation(root[:, :], veps[:, :], ACT.Sqrt).then_inc(root_done, 1)

            def normalise(b, c):
                n = G * b + c
                if isinstance(n, int) and n >= TILES:
                    return
                act.wait_ge(stats_done, 2 * n + 2)
                at_least(act, h_turned, n)
                nc.scalar.activation(h[:, :], xs[c % G][:, :], ACT.Identity, bias=shift[:, 0:1], scale=gain[:, 0:1]
                                     ).then_inc(h_done, 1)

            def high(b, c):
                n = G * b + c
                if isinstance(n, int) and n >= TILES:
                    return
                act.wait_ge(h_turned, n + 1)
                at_least(act, out_mm, OC * (n - 1))
                nc.scalar.activation(h_hi[c % 2][:, :, :], t_ps[:, :, :], ACT.Copy).then_inc(hi_done, 1)

            def step(b, c):
                take_root(b, c + 2)
                high(b, c + 1)
                normalise(b, c + 2)

            take_root(0, 0)
            normalise(0, 0)
            high(0, 0)
            take_root(0, 1)
            normalise(0, 1)
            run(act, step)

        @block.tensor
        def _(pe):
            def turn(b, c):
                n = G * b + c
                if isinstance(n, int) and n >= TILES:
                    return
                pe.wait_ge(h_done, n + 1)
                at_least(pe, lo_done, n)
                for k in range(DB):
                    last = nc.tensor.transpose(t_ps[:, k, :], h[:, k * T:(k + 1) * T], ident_sb[:, :])
                last.then_inc(h_turned, 1)

            def product(b, c, o):
                n = G * b + c
                at_least(pe, y_done, OC * (n - 1) + o + 1)
                part = slice(o * TG, (o + 1) * TG)
                for k in range(DB):
                    nc.tensor.matmul(out_ps[:, o, :], h_hi[c % 2][:, k, :], w_hi[:, part, k, :],
                                     start=(k == 0), stop=False)
                    nc.tensor.matmul(out_ps[:, o, :], h_hi[c % 2][:, k, :], w_lo[:, part, k, :],
                                     start=False, stop=False)
                    last = nc.tensor.matmul(out_ps[:, o, :], h_lo[c % 2][:, k, :], w_hi[:, part, k, :],
                                            start=False, stop=(k == DB - 1))
                last.then_inc(out_mm, 1)

            def step(b, c):
                n = G * b + c
                first = isinstance(n, int) and n == 0
                pe.wait_ge(lo_done, n + 1)
                for o in range(OC):
                    if o == 1:
                        turn(b, c + 1)
                    if first:
                        pe.wait_ge(w_in[o], 32)
                    product(b, c, o)

            pe.wait_ge(ident_in, 16)
            turn(0, 0)
            run(pe, step)

        @block.gpsimd
        def _(pool):
            def add_bias(b, c):
                n = G * b + c
                if isinstance(n, int) and n >= TILES:
                    return
                pool.wait_ge(h_done, n + 1)
                nc.gpsimd.tensor_tensor(xs[c % G][:, :], xs[c % G][:, :], bias_sb[:, :], ALU.add
                                        ).then_inc(bias_added, 1)

            def step(b, c):
                n = G * b + c
                pool.wait_ge(bias_added, n + 1)
                for o in range(OC):
                    part = slice(o * CH, (o + 1) * CH)
                    pool.wait_ge(y_done, OC * n + o + 1)
                    nc.gpsimd.tensor_tensor(xs[c % G][:, part], xs[c % G][:, part], y[o % 2][:, :], ALU.add
                                            ).then_inc(y_added, 1)
                add_bias(b, c + 2)

            pool.wait_ge(const_in, 32)
            add_bias(0, 0)
            add_bias(0, 1)
            run(pool, step)


def program(nc, x, values, W, bias, A, Bf, coeffs, scales, consts, out):
    x1 = nc.dram_tensor("x1_scratch", [BATCH, L, D], F32, kind="Internal").ap()
    whi = nc.dram_tensor("whi_scratch", [T, OT, DB, T], F16, kind="Internal").ap()
    wlo = nc.dram_tensor("wlo_scratch", [T, OT, DB, T], F16, kind="Internal").ap()
    wscale = nc.dram_tensor("wscale_scratch", [D], F32, kind="Internal").ap()
    with ExitStack() as ctx:
        shared = Shared(nc, ctx, x, values, consts)
        prepare(nc, shared, x, W, A, Bf, coeffs, scales, whi, wlo, wscale)
        attend(nc, shared, x, x1)
    feed(nc, x1, bias, whi, wlo, wscale, consts["ident"], out)


_INS = ["x", "ctx_4096", "L0_ffn_W", "L0_ffn_bias", "L0_ffn_A", "L0_ffn_Bf", "L0_ffn_coeffs", "L0_ffn_scales"]


def kernel(**inputs):
    import concourse.bacc as _bacc
    from concourse.bass_utils import run_bass_kernel_spmd as _run

    nc = _bacc.Bacc("TRN2", target_bir_lowering=False, num_devices=1, dynamic_dma_scratch_size=4096)
    arrays, args, consts = {}, [], {}
    for name in _INS:
        a = np.asarray(inputs[name])
        if name in ("x", "ctx_4096"):
            a = a[:, position_order()]
        a = np.ascontiguousarray(a)
        arrays[f"in_{name}_dram"] = a
        args.append(nc.dram_tensor(f"in_{name}_dram", a.shape, mybir.dt.from_np(a.dtype), kind="ExternalInput").ap())
    for name, a in transform_matrices().items():
        a = np.ascontiguousarray(a.astype(np.float32))
        arrays[f"const_{name}_dram"] = a
        consts[name] = nc.dram_tensor(f"const_{name}_dram", a.shape, F32, kind="ExternalInput").ap()
    out = nc.dram_tensor("out_0_dram", (BATCH, L, D), F32, kind="ExternalOutput").ap()
    program(nc, *args, consts, out)
    r = _run(nc, [arrays], core_ids=[0])
    return r.results[0]["out_0_dram"][:, np.argsort(position_order())]
```
